# Optimizing a Trainium2 kernel written in Bass

```python
import numpy as np
import jax
import jax.numpy as jnp

def _softmax(x, axis=-1):
    return jax.nn.softmax(x, axis=axis)

def _gelu(x):
    return jax.nn.gelu(x, approximate=True)

def _silu(x):
    return jax.nn.silu(x)

def _sigmoid(x):
    return jax.nn.sigmoid(x)

def _layernorm(x, axis=-1, eps=1e-05):
    m = jnp.mean(x, axis=axis, keepdims=True)
    v = jnp.var(x, axis=axis, keepdims=True)
    return (x - m) / jnp.sqrt(v + eps)

def _scatter_add(tgt, idx, src, axis=0):
    return tgt.at[idx].add(src)

def _segment_sum(src, seg, n):
    return jax.ops.segment_sum(src, seg, n)
kernel_name = 'mk_macaron_d1_jaxref_r8_faa847'

def setup_inputs(seed: int=0):
    np.random.seed(seed)
    _w = jnp.asarray

    def _L0_attn_setup():
        import jax, jax.numpy as jnp
        import numpy as np
        NUM_HEADS = 16
        EMBED_DIM = 128
        HEAD_DIM = EMBED_DIM // NUM_HEADS

        def _split_heads(t):
            b, s, _ = t.shape
            return t.reshape(b, s, NUM_HEADS, HEAD_DIM).transpose(0, 2, 1, 3)
        key = jax.random.key(seed)
        ks = jax.random.split(key, 5)
        scale = 1.0 / np.sqrt(EMBED_DIM)
        return {'x': jax.random.normal(ks[0], (2, 256, EMBED_DIM), dtype=jnp.float32), 'q_proj': jax.random.normal(ks[1], (EMBED_DIM, EMBED_DIM), dtype=jnp.float32) * scale, 'k_proj': jax.random.normal(ks[2], (EMBED_DIM, EMBED_DIM), dtype=jnp.float32) * scale, 'v_proj': jax.random.normal(ks[3], (EMBED_DIM, EMBED_DIM), dtype=jnp.float32) * scale, 'out_proj': jax.random.normal(ks[4], (EMBED_DIM, EMBED_DIM), dtype=jnp.float32) * scale}
    _L0_attn_in = _L0_attn_setup()

    def _L0_ffn_setup():
        import jax, jax.numpy as jnp
        import numpy as np
        TOP_K = 2
        N_EXPERTS = 8
        key = jax.random.key(seed)
        k_x, k_g, k_w1, k_w2 = jax.random.split(key, 4)
        B, S, d_in, d_hid, d_out, E = (8, 256, 128, 256, 128, N_EXPERTS)
        s_gate = float(np.sqrt(6.0 / (d_in + E)))
        s_w1 = float(np.sqrt(6.0 / (d_in + d_hid)))
        s_w2 = float(np.sqrt(6.0 / (d_hid + d_out)))
        x = jax.random.normal(k_x, (B, S, d_in), dtype=jnp.float32)
        gate_W = jax.random.uniform(k_g, (d_in, E), jnp.float32, -s_gate, s_gate)
        W1 = jax.random.uniform(k_w1, (E, d_in, d_hid), jnp.float32, -s_w1, s_w1)
        b1 = jnp.zeros((E, d_hid), jnp.float32)
        W2 = jax.random.uniform(k_w2, (E, d_hid, d_out), jnp.float32, -s_w2, s_w2)
        b2 = jnp.zeros((E, d_out), jnp.float32)
        return {'x': x, 'gate_W': gate_W, 'W1': W1, 'b1': b1, 'W2': W2, 'b2': b2}
    _L0_ffn_in = _L0_ffn_setup()
    _d = {'L0_attn_x': _L0_attn_in['x'], 'L0_attn_q_proj': _L0_attn_in['q_proj'], 'L0_attn_k_proj': _L0_attn_in['k_proj'], 'L0_attn_v_proj': _L0_attn_in['v_proj'], 'L0_attn_out_proj': _L0_attn_in['out_proj'], 'L0_ffn_gate_W': _L0_ffn_in['gate_W'], 'L0_ffn_W1': _L0_ffn_in['W1'], 'L0_ffn_b1': _L0_ffn_in['b1'], 'L0_ffn_W2': _L0_ffn_in['W2'], 'L0_ffn_b2': _L0_ffn_in['b2']}
    _x0 = _d['L0_attn_x']
    _d['L0_attn_x'] = jax.random.normal(jax.random.fold_in(jax.random.key(seed), 1), (32, 256, 128), dtype=_x0.dtype)
    del _x0
    return _d

def reference(L0_attn_x, L0_attn_q_proj, L0_attn_k_proj, L0_attn_v_proj, L0_attn_out_proj, L0_ffn_gate_W, L0_ffn_W1, L0_ffn_b1, L0_ffn_W2, L0_ffn_b2):

    def _L0_attn_ref(x, q_proj, k_proj, v_proj, out_proj):
        import jax, jax.numpy as jnp
        import numpy as np
        NUM_HEADS = 16
        EMBED_DIM = 128
        HEAD_DIM = EMBED_DIM // NUM_HEADS

        def _split_heads(t):
            b, s, _ = t.shape
            return t.reshape(b, s, NUM_HEADS, HEAD_DIM).transpose(0, 2, 1, 3)
        q = _split_heads(x @ q_proj)
        k = _split_heads(x @ k_proj)
        v = _split_heads(x @ v_proj)
        scale = 1.0 / np.sqrt(HEAD_DIM).astype(np.float32)
        scores = jnp.einsum('bhid,bhjd->bhij', q, k) * scale
        s = scores.shape[-1]
        causal = jnp.tril(jnp.ones((s, s), dtype=bool))
        scores = jnp.where(causal, scores, jnp.float32(-jnp.inf))
        probs = jax.nn.softmax(scores, axis=-1)
        ctx = jnp.einsum('bhij,bhjd->bhid', probs, v)
        b = ctx.shape[0]
        ctx = ctx.transpose(0, 2, 1, 3).reshape(b, s, EMBED_DIM)
        return ctx @ out_proj

    def _L0_ffn_ref(x, gate_W, W1, b1, W2, b2):
        import jax, jax.numpy as jnp
        import numpy as np
        TOP_K = 2
        N_EXPERTS = 8
        E = W1.shape[0]
        d_in = x.shape[-1]
        d_out = W2.shape[-1]
        x_flat = x.reshape(-1, d_in)
        logits = x_flat @ gate_W
        gates = jax.nn.softmax(logits, axis=-1)
        tk_g, tk_i = jax.lax.top_k(gates, TOP_K)
        tk_g = tk_g / (jnp.sum(tk_g, axis=-1, keepdims=True) + 1e-08)
        cw = jnp.sum(jax.nn.one_hot(tk_i, E, dtype=x.dtype) * tk_g[..., None], axis=1)
        out = x_flat
        for e in range(E):
            h = jax.nn.relu(x_flat @ W1[e] + b1[e])
            out = out + cw[:, e:e + 1] * (h @ W2[e] + b2[e])
        return out.reshape(x.shape[:-1] + (d_out,))
    x = L0_attn_x
    x = x + 0.5 * _L0_ffn_ref(_layernorm(x, axis=-1), L0_ffn_gate_W, L0_ffn_W1, L0_ffn_b1, L0_ffn_W2, L0_ffn_b2)
    x = x + _L0_attn_ref(_layernorm(x, axis=-1), L0_attn_q_proj, L0_attn_k_proj, L0_attn_v_proj, L0_attn_out_proj)
    x = x + 0.5 * _L0_ffn_ref(_layernorm(x, axis=-1), L0_ffn_gate_W, L0_ffn_W1, L0_ffn_b1, L0_ffn_W2, L0_ffn_b2)
    return x

_drawn_inputs = setup_inputs


def setup_inputs(seed=0):
    import zlib

    import numpy as np

    out = dict(_drawn_inputs(seed))
    spreads = {'L0_ffn_b1': (0.0, 0.1), 'L0_ffn_b2': (0.0, 0.1)}
    factors = {}
    for name, (base, spread) in spreads.items():
        noise = np.random.default_rng([zlib.crc32(name.encode()), seed]).standard_normal(out[name].shape)
        drawn = base * np.exp(spread * noise) if base else spread * noise
        out[name] = jnp.asarray(drawn.astype(out[name].dtype))
    for name, factor in factors.items():
        out[name] = (out[name] * factor).astype(out[name].dtype)
    return out
```

```python
import concourse.bass as bass
from concourse import mybir
from contextlib import ExitStack


fp32 = mybir.dt.float32
fp16 = mybir.dt.float16
bf16 = mybir.dt.bfloat16
ALU = mybir.AluOpType
ACT = mybir.ActivationFunctionType
AX = mybir.AxisListType

P = 128
NB, SEQ, D = 32, 256, 128
NBLK = NB * SEQ // P
E, HID = 8, 256
HC = HID // P
TB = 4
TT = TB * P
NT = NBLK // TB
H, HD = 16, 8
NG, GH = 4, 4
SB = SEQ // P
EPS = 1e-5
WSCALE = 64.0
BIG = -1.0e30


def ds(start, size):
    return bass.ds(start, size)


def take(eng, sem, n=1):
    eng.wait_ge(sem, n)
    eng.sem_inc(sem, -n)


def link(eng, sem, ins):
    ins.then_inc(sem, 1)
    take(eng, sem)


def build(nc, x_in, q_proj, k_proj, v_proj, out_proj, gate_w, w1, b1, w2, b2, out):
    xin_v = x_in.rearrange("b (k p) d -> p (b k) d", p=P)
    out_v = out.rearrange("b (k p) d -> p (b k) d", p=P)
    with ExitStack() as ctx:
        def sb(name, shape, dt):
            return ctx.enter_context(nc.sbuf_tensor(name, shape, dt))

        def sem(name):
            return ctx.enter_context(nc.semaphore(name))

        x = sb("x", [P, NBLK * D], fp32)
        ident = sb("ident", [P, P], fp32)
        ident_h = sb("ident_h", [P, P], fp16)
        ident_b = sb("ident_b", [P, P], bf16)
        gw = sb("gw", [P, E], fp32)
        w1f = sb("w1f", [P, E, HID], fp32)
        w1h = sb("w1h", [P, E, HID], fp16)
        w1l = sb("w1l", [P, E, HID], fp16)
        w2f = sb("w2f", [P, E * HC, D], fp32)
        b1r = sb("b1r", [E * HC, P], fp32)
        b1c = sb("b1c", [P, E * HC], fp32)
        b2s = sb("b2s", [E, D], fp32)
        wq = sb("wq", [P, D], fp32)
        wk = sb("wk", [P, D], fp32)
        wv = sb("wv", [P, D], fp32)
        wo = sb("wo", [P, D], fp32)
        mask = sb("mask", [P, GH, P], bf16)
        neg_half = sb("neg_half", [P, TB], fp32)
        order = sb("order", [P, TB, E], fp32)
        ps = [ctx.enter_context(nc.psum_tensor(f"bank{i}", [P, 512], fp32)) for i in range(8)]

        xdone = sem("x_loaded")
        setup(nc, ctx, sem, x, xin_v, xdone, ps, ident, ident_h, ident_b, gw, w1f, w1h, w1l, w2f, b1r,
              b1c, b2s, wq, wk, wv, wo, mask, neg_half, order,
              gate_w, w1, b1, w2, b2, q_proj, k_proj, v_proj, out_proj)
        with ExitStack() as part:
            ffn_phase(nc, part, "f1", x, xin_v, xdone, ps, ident, gw, w1h, w1l, w2f, b1c, b2s, neg_half, order, None)
        with ExitStack() as part:
            attention_phase(nc, part, x, ps, ident, ident_h, ident_b, mask, neg_half, wq, wk, wv, wo)
        with ExitStack() as part:
            ffn_phase(nc, part, "f2", x, None, None, ps, ident, gw, w1h, w1l, w2f, b1c, b2s, neg_half, order, out_v)


def setup(nc, ctx, sem, x, xin_v, xdone, ps, ident, ident_h, ident_b, gw, w1f, w1h, w1l, w2f, b1r,
          b1c, b2s, wq, wk, wv, wo, mask, neg_half, order,
          gate_w, w1, b1, w2, b2, q_proj, k_proj, v_proj, out_proj):
    w_in = [sem(f"w_in{i}") for i in range(5)]
    ident_z = sem("ident_z")
    ident_r = sem("ident_r")
    mask_z = sem("mask_z")
    b1_t = sem("b1_t")
    split = sem("w1_split")
    casts = sem("const_casts")
    with nc.Block() as block:
        @block.sync
        def _(sp):
            sp.dma_start(x[:, 0:TT].rearrange("p (k d) -> p k d", d=D), xin_v[:, 0:TB, :]).then_inc(xdone, 16)
            sp.dma_start(w1f[:], w1.rearrange("e d h -> d e h")).then_inc(w_in[0], 16)
            sp.dma_start(b1r[:], b1.rearrange("e (c p) -> (e c) p", p=P)).then_inc(w_in[2], 16)
            sp.dma_start(gw[:], gate_w).then_inc(w_in[3], 16)
            sp.dma_start(b2s[:], b2).then_inc(w_in[3], 16)
            sp.dma_start(w2f[:], w2.rearrange("e (c p) o -> p (e c) o", p=P)).then_inc(w_in[1], 16)
            for dst, src in ((wq, q_proj), (wk, k_proj), (wv, v_proj), (wo, out_proj)):
                sp.dma_start(dst[:], src).then_inc(w_in[4], 16)
            sp.wait_ge(xdone, 16)
            for s, n in zip(w_in, (16, 16, 16, 32, 64)):
                sp.wait_ge(s, n)

        @block.gpsimd
        def _(pool):
            nc.gpsimd.memset(ident[:], 0.0).then_inc(ident_z, 1)
            nc.gpsimd.memset(mask[:], 0.0).then_inc(mask_z, 1)
            nc.gpsimd.memset(neg_half[:], -0.5)
            for e in range(E):
                nc.gpsimd.memset(order[:, :, e], float(E - e))
            pool.wait_ge(ident_z, 1)
            nc.gpsimd.affine_select(out=ident[:], in_=ident[:], compare_op=ALU.not_equal, fill=1.0, base=0,
                                    pattern=[[-1, P]], channel_multiplier=1).then_inc(ident_r, 1)
            pool.wait_ge(mask_z, 1)
            nc.gpsimd.affine_select(out=mask[:], in_=mask[:], compare_op=ALU.is_ge, fill=BIG, base=0,
                                    pattern=[[0, GH], [-1, P]], channel_multiplier=1)

        @block.tensor
        def _(pe):
            pe.wait_ge(ident_r, 1)
            pe.wait_ge(w_in[2], 16)
            nc.tensor.transpose(ps[0][:, 0:E * HC], b1r[:], ident[0:E * HC, 0:E * HC]).then_inc(b1_t, 1)

        @block.scalar
        def _(act):
            act.wait_ge(w_in[0], 16)
            nc.scalar.activation(w1h[:], w1f[:], ACT.Copy, scale=WSCALE).then_inc(split, 1)

        @block.vector
        def _(dve):
            dve.wait_ge(ident_r, 1)
            nc.vector.tensor_copy(ident_h[:], ident[:])
            nc.vector.tensor_copy(ident_b[:], ident[:]).then_inc(casts, 1)
            dve.wait_ge(b1_t, 1)
            nc.vector.tensor_copy(b1c[:], ps[0][:, 0:E * HC])
            dve.wait_ge(split, 1)
            nc.vector.scalar_tensor_tensor(out=w1l[:].rearrange("p e h -> p (e h)"), in0=w1f[:].rearrange("p e h -> p (e h)"), scalar=WSCALE, in1=w1h[:].rearrange("p e h -> p (e h)"),
                                           op0=ALU.mult, op1=ALU.subtract)


def ffn_phase(nc, ctx, name, x, xin_v, xdone, ps, ident, gw, w1h, w1l, w2f, b1c, b2s, neg_half, order, out_v):
    def sb(nm, shape, dt):
        return ctx.enter_context(nc.sbuf_tensor(f"{name}_{nm}", shape, dt))

    def sem(nm):
        return ctx.enter_context(nc.semaphore(f"{name}_{nm}"))

    stats = sb("stats", [P, TB, 6], fp32)
    mv = sb("mv", [P, TB, 2], fp32)
    veps = sb("veps", [P, TB], fp32)
    rstd = sb("rstd", [P, TB], fp32)
    xn = sb("xn", [P, TB, D], fp32)
    xT = [sb(f"xT{i}", [P, TT], fp32) for i in range(2)]
    xTh = [sb(f"xTh{i}", [P, TT], fp16) for i in range(2)]
    xTl = [sb(f"xTl{i}", [P, TT], fp16) for i in range(2)]
    small = sb("small", [P, 10, TB], fp32)
    wide = sb("wide", [P, 10, TB, E], fp32)
    cw = [sb(f"cw{i}", [P, TB, E], fp32) for i in range(2)]
    cwT = sb("cwT", [E, TT], fp32)
    h = [sb(f"h{i}", [P, HC, TT], fp32) for i in range(2)]
    scaled = [sb(f"scaled{i}", [P, TT], fp32) for i in range(2)]
    b_x, b_gate, b_bias = ps[0], ps[1], ps[2]
    b_z, b_y = ps[3:5], ps[5:7]

    s_var = sem("var")
    s_rstd = sem("rstd")
    s_xn = sem("xn")
    s_tr = sem("tr")
    s_xT = sem("xT")
    s_xTl = sem("xTl")
    s_logit = sem("logit")
    s_shift = sem("shift")
    s_exp = sem("exp")
    s_cw = sem("cw")
    s_cwp = sem("cwp")
    s_cwT = sem("cwT")
    s_bias = sem("bias")
    s_init = sem("init")
    s_z = sem("z")
    s_h = sem("h")
    s_y = sem("y")
    s_sc = sem("sc")
    s_acc = sem("acc")
    s_dve = sem("dve")

    tiles = x[:]

    def pe_front(pe, t, par, step):
        if step == 0:
            pe.wait_ge(s_xn, t + 1)
            for j in range(TB):
                last = nc.tensor.transpose(b_x[:, j * P:(j + 1) * P], xn[:, j, :], ident[:])
            last.then_inc(s_tr, 1)
        if step == 1:
            pe.wait_ge(s_xT, t + 1)
            for j in range(TB):
                last = nc.tensor.matmul(b_gate[:, j * E:(j + 1) * E], xT[par][:, j * P:(j + 1) * P], gw[:],
                                        start=True, stop=True)
            last.then_inc(s_logit, 1)
        if step == 2:
            pe.wait_ge(s_cw, t + 1)
            for j in range(TB):
                last = nc.tensor.transpose(b_gate[0:E, j * P:(j + 1) * P], cw[par][:, j, :], ident[:])
            last.then_inc(s_cwp, 1)
        if step == 3:
            pe.wait_ge(s_cwT, t + 1)
            for j in range(TB):
                last = nc.tensor.matmul(b_bias[:, j * P:(j + 1) * P], cwT[:, j * P:(j + 1) * P], b2s[:],
                                        start=True, stop=True)
            last.then_inc(s_bias, 1)

    def pe_first(pe, t, par, e):
        for c in range(HC):
            pe.wait_ge(s_h, t * 16 + (2 * e + c + 1))
            z = b_z[c][:, :]
            w = slice(c * P, (c + 1) * P)
            nc.tensor.matmul(z, w1h[:, e, w], xTh[par][:], start=True, stop=False)
            nc.tensor.matmul(z, w1l[:, e, w], xTh[par][:], start=False, stop=False)
            nc.tensor.matmul(z, w1h[:, e, w], xTl[par][:], start=False, stop=True).then_inc(s_z, 1)

    def pe_second(pe, t, par, e):
        pe.wait_ge(s_h, t * 16 + (2 * e + 2 + 2))
        pe.wait_ge(s_acc, t * 8 + (e + 1))
        for j in range(TB):
            for c in range(HC):
                last = nc.tensor.matmul(b_y[e % 2][:, j * P:(j + 1) * P], h[e % 2][:, c, j * P:(j + 1) * P],
                                        w2f[:, e * HC + c, :], start=(c == 0), stop=(c == HC - 1))
        last.then_inc(s_y, 1)

    def pe_tile(pe, t, par, more):
        pe.wait_ge(s_xTl, t + 1)
        pe_first(pe, t, par, 0)
        for e in range(1, E):
            pe_first(pe, t, par, e)
            pe_second(pe, t, par, e - 1)
            if more and e == 3:
                pe_front(pe, t + 1, 1 - par, 0)
            if more and e == 4:
                pe_front(pe, t + 1, 1 - par, 1)
            if more and e == 7:
                pe_front(pe, t + 1, 1 - par, 2)
        pe_second(pe, t, par, E - 1)
        if more:
            pe_front(pe, t + 1, 1 - par, 3)

    def act_front(act, t, par, step):
        if step == 0:
            act.wait_ge(s_tr, t + 1)
            nc.scalar.copy(xTh[par][:], b_x[:, :])
            nc.scalar.copy(xT[par][:], b_x[:, :]).then_inc(s_xT, 1)
        if step == 1:
            act.wait_ge(s_shift, t + 1)
            nc.scalar.activation(wide[:, 1], wide[:, 0], ACT.Exp).then_inc(s_exp, 1)

    def act_tile(act, t, par, more):
        for e in range(E):
            act.wait_ge(s_y, t * 8 + (e + 1))
            for c in range(HC):
                act.wait_ge(s_z, t * 16 + (2 * e + c + 1))
                nc.scalar.activation(h[e % 2][:, c, :], b_z[c][:, :], ACT.Relu, scale=1.0 / WSCALE,
                                     bias=b1c[:, e * HC + c:e * HC + c + 1]).then_inc(s_h, 1)
            if more and e == 3:
                act_front(act, t + 1, 1 - par, 0)
            if more and e == 5:
                act_front(act, t + 1, 1 - par, 1)

    def dve_front(dve, t, par, step):
        S, W = small, wide

        def row(i):
            return S[:, i, :]

        def over(i):
            return S[:, i, :].unsqueeze(2).to_broadcast([P, TB, E])

        if step == 0:
            if xdone is not None:
                dve.wait_ge(xdone, t * 16 + 16)
            for j in range(TB):
                last = nc.vector.bn_stats(stats[:, j, :], x[:, ds(t * TT + j * P, P)])
            link(dve, s_dve, last)
            for j in range(TB):
                last = nc.vector.bn_aggr(mv[:, j, :], stats[:, j, :])
            link(dve, s_dve, last)
            nc.vector.tensor_scalar_add(veps[:], mv[:, :, 1], EPS).then_inc(s_var, 1)
        if step == 1:
            dve.wait_ge(s_rstd, t + 1)
            for j in range(TB):
                last = nc.vector.tensor_scalar(xn[:, j, :], x[:, ds(t * TT + j * P, P)], mv[:, j, 0:1],
                                               rstd[:, j:j + 1], ALU.subtract, ALU.mult)
            last.then_inc(s_xn, 1)
        if step == 2:
            dve.wait_ge(s_xT, t + 1)
            nc.vector.tensor_tensor(xTl[par][:], xT[par][:], xTh[par][:], ALU.subtract).then_inc(s_xTl, 1)
        if step == 3:
            lg = b_gate[:, 0:TB * E].rearrange("p (j e) -> p j e", e=E)
            dve.wait_ge(s_logit, t + 1)
            link(dve, s_dve, nc.vector.reduce_max(row(0), lg, AX.X))
            nc.vector.tensor_tensor(W[:, 0], lg, over(0), ALU.subtract).then_inc(s_shift, 1)
        if step == 4:
            dve.wait_ge(s_exp, t + 1)
            link(dve, s_dve, nc.vector.reduce_sum(row(1), W[:, 1], AX.X))
            link(dve, s_dve, nc.vector.reciprocal(row(2), row(1)))
            link(dve, s_dve, nc.vector.tensor_tensor(W[:, 2], W[:, 1], over(2), ALU.mult))
            link(dve, s_dve, nc.vector.reduce_max(row(3), W[:, 2], AX.X))
            link(dve, s_dve, nc.vector.tensor_tensor(W[:, 3], W[:, 2], over(3), ALU.is_equal))
            link(dve, s_dve, nc.vector.tensor_tensor(W[:, 4], W[:, 3], order[:], ALU.mult))
            link(dve, s_dve, nc.vector.reduce_max(row(4), W[:, 4], AX.X))
            link(dve, s_dve, nc.vector.tensor_tensor(W[:, 5], W[:, 4], over(4), ALU.is_equal))
            link(dve, s_dve, nc.vector.scalar_tensor_tensor(out=W[:, 6], in0=W[:, 5], scalar=-2.0, in1=W[:, 2],
                                                   op0=ALU.mult, op1=ALU.add))
            link(dve, s_dve, nc.vector.reduce_max(row(5), W[:, 6], AX.X))
            link(dve, s_dve, nc.vector.tensor_tensor(W[:, 7], W[:, 6], over(5), ALU.is_equal))
            link(dve, s_dve, nc.vector.tensor_tensor(W[:, 8], W[:, 7], order[:], ALU.mult))
            link(dve, s_dve, nc.vector.reduce_max(row(6), W[:, 8], AX.X))
            link(dve, s_dve, nc.vector.tensor_tensor(W[:, 9], W[:, 8], over(6), ALU.is_equal))
            link(dve, s_dve, nc.vector.scalar_tensor_tensor(out=row(7), in0=row(3), scalar=1e-8, in1=row(5),
                                                   op0=ALU.add, op1=ALU.add))
            link(dve, s_dve, nc.vector.reciprocal(row(8), row(7)))
            link(dve, s_dve, nc.vector.tensor_tensor(W[:, 3], W[:, 5], W[:, 9], ALU.add))
            link(dve, s_dve, nc.vector.tensor_tensor(W[:, 4], W[:, 2], W[:, 3], ALU.mult))
            nc.vector.scalar_tensor_tensor(out=cw[par][:], in0=W[:, 4], scalar=0.5, in1=over(8),
                                           op0=ALU.mult, op1=ALU.mult).then_inc(s_cw, 1)
        if step == 5:
            dve.wait_ge(s_cwp, t + 1)
            nc.vector.tensor_copy(cwT[:], b_gate[0:E, :]).then_inc(s_cwT, 1)
        if step == 6:
            xs = x[:, ds(t * TT, TT)]
            link(dve, s_dve, nc.vector.scalar_tensor_tensor(out=xs, in0=xn[:].rearrange("p j d -> p (j d)"), scalar=0.5,
                                                   in1=xs, op0=ALU.mult, op1=ALU.add))
            dve.wait_ge(s_bias, t + 1)
            nc.vector.tensor_tensor(xs, b_bias[:, :], xs, ALU.add).then_inc(s_init, 1)

    def dve_scale(dve, t, par, e):
        dve.wait_ge(s_y, t * 8 + (e + 1 + 2))
        dve.wait_ge(s_acc, t * 8 + (e + 1))
        nc.vector.tensor_tensor(scaled[e % 2][:].rearrange("p (j d) -> p j d", d=D),
                                b_y[e % 2][:, :].rearrange("p (j d) -> p j d", d=D),
                                cw[par][:, :, e:e + 1].to_broadcast([P, TB, D]), ALU.mult).then_inc(s_sc, 1)

    def dve_tile(dve, t, par, more):
        if more:
            dve_front(dve, t + 1, 1 - par, 0)
        for e in range(E):
            dve_scale(dve, t, par, e)
            if more:
                for step, at in ((1, 0), (2, 2), (3, 3), (4, 4), (5, 6), (6, 7)):
                    if e == at:
                        dve_front(dve, t + 1, 1 - par, step)

    def pool_front(pool, t):
        take(pool, s_var)
        nc.gpsimd.tensor_tensor(rstd[:], veps[:], neg_half[:], ALU.pow).then_inc(s_rstd, 1)

    def pool_tile(pool, t, more):
        if more:
            pool_front(pool, t + 1)
        take(pool, s_init)
        xs = x[:, ds(t * TT, TT)]
        for e in range(E):
            pool.wait_ge(s_acc, t * 8 + (e + 2))
            take(pool, s_sc)
            nc.gpsimd.tensor_tensor(xs, xs, scaled[e % 2][:], ALU.add).then_inc(s_acc, 1)

    with nc.Block() as block:
        @block.sync
        def _(sp):
            if xdone is not None:
                with sp.Fori(1, NT) as t:
                    sp.wait_ge(xdone, t * 16)
                    sp.dma_start(x[:, ds(t * TT, TT)].rearrange("p (k d) -> p k d", d=D),
                                 xin_v[:, ds(t * TB, TB), :]).then_inc(xdone, 16)
            if out_v is not None:
                s_out = sem("out")
                with sp.Fori(0, NT) as t:
                    sp.wait_ge(s_acc, t * 8 + (8 + 2))
                    sp.dma_start(out_v[:, ds(t * TB, TB), :],
                                 x[:, ds(t * TT, TT)].rearrange("p (k d) -> p k d", d=D)).then_inc(s_out, 16)
                sp.wait_ge(s_out, NT * 16)

        @block.tensor
        def _(pe):
            pe.sem_inc(s_y, 2)
            for step in range(4):
                pe_front(pe, 0, 0, step)
            with pe.Fori(0, NT - 2, 2) as t:
                pe_tile(pe, t, 0, True)
                pe_tile(pe, t + 1, 1, True)
            pe_tile(pe, NT - 2, 0, True)
            pe_tile(pe, NT - 1, 1, False)

        @block.scalar
        def _(act):
            act.sem_inc(s_h, 2)
            for step in range(2):
                act_front(act, 0, 0, step)
            with act.Fori(0, NT - 2, 2) as t:
                act_tile(act, t, 0, True)
                act_tile(act, t + 1, 1, True)
            act_tile(act, NT - 2, 0, True)
            act_tile(act, NT - 1, 1, False)

        @block.vector
        def _(dve):
            for step in range(7):
                dve_front(dve, 0, 0, step)
            with dve.Fori(0, NT - 2, 2) as t:
                dve_tile(dve, t, 0, True)
                dve_tile(dve, t + 1, 1, True)
            dve_tile(dve, NT - 2, 0, True)
            dve_tile(dve, NT - 1, 1, False)

        @block.gpsimd
        def _(pool):
            pool.sem_inc(s_acc, 2)
            pool_front(pool, 0)
            with pool.Fori(0, NT - 1) as t:
                pool_tile(pool, t, True)
            pool_tile(pool, NT - 1, False)


def attention_phase(nc, ctx, x, ps, ident, ident_h, ident_b, mask, neg_half, wq, wk, wv, wo):
    def sb(nm, shape, dt):
        return ctx.enter_context(nc.sbuf_tensor(f"at_{nm}", shape, dt))

    def sem(nm):
        return ctx.enter_context(nc.semaphore(f"at_{nm}"))

    SCALE = 1.0 / float(HD) ** 0.5
    SLOT = 3 * HD

    sel = {k: sb(f"sel_{k}", [P, NG, GH, 4, HD], fp16) for k in ("qh", "ql", "kh", "kl")}
    SLOTS = {"qh": (0, 1), "ql": (2,), "kh": (0, 2), "kl": (1,)}
    kones = sb("kones", [P, 1], fp32)
    stats = sb("stats", [P, SB, 6], fp32)
    mv = sb("mv", [P, SB, 2], fp32)
    veps = sb("veps", [P, SB], fp32)
    rstd = sb("rstd", [P, SB], fp32)
    xn = sb("xn", [P, SB, D], fp32)
    xT = sb("xT", [P, SEQ], fp32)
    qkh = sb("qkh", [P, 2, SEQ], fp16)
    qkl = sb("qkl", [P, 2, SEQ], fp16)
    qs = [sb(f"qs{i}", [P, NG, SEQ], fp16) for i in range(2)]
    ks = [sb(f"ks{i}", [P, NG, SEQ], fp16) for i in range(2)]
    va = [sb(f"va{i}", [P, SB, H, 32], fp32) for i in range(2)]
    mx = sb("mx", [P, SB, H], fp32)
    marr = sb("marr", [P, SB, NG, GH, 4 * HD], fp16)
    pt = [sb(f"pt{i}", [P, 3, 512], fp32) for i in range(2)]
    cT = [sb(f"cT{i}", [P, SEQ], fp32) for i in range(2)]
    rden = sb("rden", [P, SB, H], fp32)
    cn = sb("cn", [P, SB, D], fp32)
    cnT = sb("cnT", [P, SEQ], fp32)
    b_s, b_ring, b_pv, b_c = ps[0:3], ps[3:5], ps[5], ps[6:8]

    s_const = sem("const")
    s_zero = sem("zero")
    s_ident = sem("ident")
    s_var = sem("var")
    s_rstd = sem("rstd")
    s_xn = sem("xn")
    s_qkh = sem("qkh")
    s_stat = sem("stat")
    s_marr = sem("marr")
    s_full = [sem(f"full{i}") for i in range(2)]
    s_free = [sem(f"free{i}") for i in range(2)]
    s_s = [sem(f"s{i}") for i in range(3)]
    s_e = [sem(f"e{i}") for i in range(3)]
    s_p = [sem(f"p{i}") for i in range(3)]
    s_pv = sem("pv")
    s_cT = sem("cT")
    s_ct = sem("ct")
    s_rden = sem("rden")
    s_cn = sem("cn")
    s_cnt = sem("cnt")
    s_cnT = sem("cnT")
    s_o = sem("o")
    s_x = sem("x")

    PER = 21
    FULL = {"max": (0, 4, 8, 11), "tr": 3, "qk": 7, "m": 14, "stack": 16, "v": 20}
    LEAN = {"max": (0, 3, 6, 9), "m": 12}
    FIRST = {"tr": 0, "qk": 1, "stack": 2, "v": 6}
    START = 7 + PER
    STACK_BACK, V_BACK, M_BACK = FULL["stack"] - PER, FULL["v"] - 2 * PER, FULL["m"] - PER

    def ring(at, n):
        pairs, off = at
        return (off + n) % 2, pairs + (off + n) // 2

    def pe_take(pe, at, n):
        bank, k = ring(at, n)
        pe.wait_ge(s_free[bank], k + 1)
        return bank

    def read(eng, at, n, take=None):
        bank, k = ring(at, n)
        if take is not None and ring(at, take)[0] == bank:
            return
        eng.wait_ge(s_free[bank], k + 2)

    def pe_tr(pe, b, at, where):
        pe.wait_ge(s_xn, b + 1)
        bank = pe_take(pe, at, where["tr"])
        for j in range(SB):
            last = nc.tensor.transpose(b_ring[bank][:, j * P:(j + 1) * P], xn[:, j, :], ident[:])
        last.then_inc(s_full[bank], 1)

    def pe_qk(pe, b, at, where):
        read(pe, at, where["tr"], where["qk"])
        bank = pe_take(pe, at, where["qk"])
        for i, w in enumerate((wq, wk)):
            last = nc.tensor.matmul(b_ring[bank][:, i * SEQ:(i + 1) * SEQ], w[:], xT[:], start=True, stop=True)
        last.then_inc(s_full[bank], 1)

    def pe_stacks(pe, b, at, where):
        read(pe, at, where["qk"], where["stack"])
        for u in range(4):
            bank = pe_take(pe, at, where["stack"] + u)
            i, half = u % 2, u // 2
            for g in range(2):
                o = b_ring[bank][:, g * SEQ:(g + 1) * SEQ]
                hi, lo = (sel[k][:, 2 * half + g].rearrange("p i s d -> p (i s d)") for k in (("qh", "ql"), ("kh", "kl"))[i])
                nc.tensor.matmul(o, hi, qkh[:, i, :], start=True, stop=False)
                last = nc.tensor.matmul(o, lo, qkl[:, i, :], start=False, stop=True)
            last.then_inc(s_full[bank], 1)

    def pe_v(pe, b, at, where):
        bank = pe_take(pe, at, where["v"])
        for j in range(SB):
            last = nc.tensor.matmul(b_ring[bank][:, j * P:(j + 1) * P], xT[:, j * P:(j + 1) * P], wv[:],
                                    start=True, stop=True)
        last.then_inc(s_full[bank], 1)

    def pe_max(pe, b, par, at, where, r):
        if r == 0:
            read(pe, at, STACK_BACK + 2)
        rows = slice(32 * r, 32 * r + 32)
        for part in range(3):
            bank = pe_take(pe, at, where["max"][r] + part)
            for n, g in enumerate(range(NG) if part == 0 else (2 * part - 2, 2 * part - 1)):
                if part == 0:
                    nc.tensor.matmul(b_ring[bank][:, n * P:(n + 1) * P], qs[par][rows, g, 0:P], ks[par][rows, g, 0:P],
                                     start=True, stop=False, tile_position=(32 * r, 0), skip_group_check=True)
                else:
                    nc.tensor.matmul(b_ring[bank][:, n * SEQ:(n + 1) * SEQ], qs[par][rows, g, P:SEQ],
                                     ks[par][rows, g, :], start=True, stop=False, tile_position=(32 * r, 0),
                                     skip_group_check=True)
            if part == 0:
                o, m = b_ring[bank][:, :], mask[:].rearrange("p i k -> p (i k)")
            else:
                o = b_ring[bank][:, :].rearrange("p (i k) -> p i k", k=SEQ)[:, :, P:SEQ]
                m = mask[:, 0:2, :]
            nc.tensor.matmul(o, ident_b[:], m, start=False, stop=True,
                             skip_group_check=True).then_inc(s_full[bank], 1)

    def pe_m(pe, b, at, where):
        pe.wait_ge(s_marr, b + 1)
        for u in range(2):
            bank = pe_take(pe, at, where["m"] + u)
            for g in range(2):
                for j in range(SB):
                    o = b_ring[bank][:, g * SEQ + j * P:g * SEQ + (j + 1) * P]
                    last = nc.tensor.matmul(o, marr[:, j, 2 * u + g].rearrange("p i r -> p (i r)"), ident_h[:],
                                            start=True, stop=True)
            last.then_inc(s_full[bank], 1)

    def pe_scores(pe, b, par, at, r, m_back):
        if r == 0:
            for u in range(2):
                read(pe, at, m_back + u)
        rows = slice(32 * r, 32 * r + 32)
        for part in range(3):
            pe.wait_ge(s_p[part], b * 4 + (r + 1))
            for n, g in enumerate(range(NG) if part == 2 else (2 * part, 2 * part + 1)):
                if part == 2:
                    last = nc.tensor.matmul(b_s[part][:, n * P:(n + 1) * P], ks[par][rows, g, P:SEQ],
                                            qs[par][rows, g, P:SEQ], start=True, stop=True, tile_position=(32 * r, 0))
                else:
                    last = nc.tensor.matmul(b_s[part][:, n * SEQ:(n + 1) * SEQ], ks[par][rows, g, 0:P],
                                            qs[par][rows, g, :], start=True, stop=True, tile_position=(32 * r, 0))
            last.then_inc(s_s[part], 1)

    def pe_pv(pe, b, par, at, g):
        if g == 0:
            read(pe, at, V_BACK)
        for part in range(3):
            pe.wait_ge(s_p[part], b * 4 + (g + 1 + 1))
        pe.wait_ge(s_cT, b * 4 + (g + 1))
        for i in range(GH):
            o = b_pv[32 * i:32 * i + 32, 0:SEQ]
            first = pt[g % 2][:, i // 2, (i % 2) * SEQ:(i % 2 + 1) * SEQ]
            nc.tensor.matmul(o, va[par][:, 0, GH * i + g, :], first, start=True, stop=False,
                             tile_position=(0, 32 * i), skip_group_check=True)
        for i in range(GH):
            o = b_pv[32 * i:32 * i + 32, P:SEQ]
            last = nc.tensor.matmul(o, va[par][:, 1, GH * i + g, :], pt[g % 2][:, 2, i * P:(i + 1) * P],
                                    start=False, stop=True, tile_position=(0, 32 * i), skip_group_check=True)
        last.then_inc(s_pv, 1)

    def pe_ct(pe, b, g):
        pe.wait_ge(s_cT, b * 4 + (g + 1 + 1))
        if g == 0:
            pe.wait_ge(s_x, b + 1)
        for j in range(SB):
            last = nc.tensor.transpose(b_c[j][:, g * P:(g + 1) * P], cT[g % 2][:, j * P:(j + 1) * P], ident[:])
        last.then_inc(s_ct, 1)

    def pe_tail_a(pe, b):
        pe.wait_ge(s_cn, b + 1)
        for j in range(SB):
            last = nc.tensor.transpose(b_c[0][:, j * P:(j + 1) * P], cn[:, j, :], ident[:])
        last.then_inc(s_cnt, 1)

    def pe_tail_b(pe, b):
        pe.wait_ge(s_cnT, b + 1)
        for j in range(SB):
            last = nc.tensor.matmul(b_c[1][:, j * P:(j + 1) * P], cnT[:, j * P:(j + 1) * P], wo[:],
                                    start=True, stop=True)
        last.then_inc(s_o, 1)

    def pe_step(pe, b, par, at, where, tail=True, here=True, maxima=True, proj=True, m_back=M_BACK):
        if maxima:
            pe_max(pe, b + 1, 1 - par, at, where, 0)
        if here:
            pe_scores(pe, b, par, at, 0, m_back)
        if tail:
            pe_tail_a(pe, b - 1)
        if proj and where is FULL:
            pe_tr(pe, b + 2, at, where)
        if maxima:
            pe_max(pe, b + 1, 1 - par, at, where, 1)
        if here:
            pe_scores(pe, b, par, at, 1, m_back)
        if tail:
            pe_tail_b(pe, b - 1)
        if here:
            pe_pv(pe, b, par, at, 0)
        if proj and where is FULL:
            pe_qk(pe, b + 2, at, where)
        if maxima:
            pe_max(pe, b + 1, 1 - par, at, where, 2)
        if here:
            pe_scores(pe, b, par, at, 2, m_back)
            pe_pv(pe, b, par, at, 1)
            pe_ct(pe, b, 0)
        if maxima:
            pe_max(pe, b + 1, 1 - par, at, where, 3)
        if here:
            pe_scores(pe, b, par, at, 3, m_back)
            pe_pv(pe, b, par, at, 2)
            pe_ct(pe, b, 1)
        if maxima:
            pe_m(pe, b + 1, at, where)
        if proj:
            if where is not FULL:
                pe_tr(pe, b + 2, at, where)
                pe_qk(pe, b + 2, at, where)
            pe_stacks(pe, b + 2, at, where)
        if here:
            pe_pv(pe, b, par, at, 3)
            pe_ct(pe, b, 2)
        if proj:
            pe_v(pe, b + 2, at, where)
        if here:
            pe_ct(pe, b, 3)

    def wait_full(eng, at, n):
        bank, k = ring(at, n)
        eng.wait_ge(s_full[bank], k + 1)
        return bank

    def act_exp(act, b, g):
        act.wait_ge(s_pv, b * 4 + (g + 1))
        for part in range(3):
            act.wait_ge(s_s[part], b * 4 + (g + 1))
            nc.scalar.activation(pt[g % 2][:, part, :], b_s[part][:, :], ACT.Exp,
                                 scale=SCALE).then_inc(s_e[part], 1)

    def act_cT(act, b, g):
        act.wait_ge(s_pv, b * 4 + (g + 1 + 2))
        act.wait_ge(s_ct, b * 4 + (g + 1))
        nc.scalar.copy(cT[g % 2][:], b_pv[:, 0:SEQ]).then_inc(s_cT, 1)

    def act_tail(act, b):
        act.wait_ge(s_cnt, b + 1)
        nc.scalar.copy(cnT[:], b_c[0][:, 0:SEQ]).then_inc(s_cnT, 1)

    def act_tr(act, b, at, where):
        bank = wait_full(act, at, where["tr"])
        nc.scalar.copy(xT[:], b_ring[bank][:, 0:SEQ]).then_inc(s_free[bank], 1)

    def act_qk(act, b, at, where):
        bank = wait_full(act, at, where["qk"])
        nc.scalar.copy(qkh[:].rearrange("p a t -> p (a t)"), b_ring[bank][:, :]).then_inc(s_qkh, 1)

    def act_stacks(act, b, par, at, where):
        for u in range(4):
            bank = wait_full(act, at, where["stack"] + u)
            i, half = u % 2, u // 2
            if i == 0:
                nc.scalar.copy(qs[par][:, 2 * half:2 * half + 2, :].rearrange("p g t -> p (g t)"),
                               b_ring[bank][:, :]).then_inc(s_free[bank], 1)
            else:
                nc.scalar.activation(ks[par][:, 2 * half:2 * half + 2, :].rearrange("p g t -> p (g t)"),
                                     b_ring[bank][:, :], ACT.Identity, bias=kones[:, 0:1]).then_inc(s_free[bank], 1)

    def act_step(act, b, par, at, where, tail=True, here=True, maxima=True, proj=True):
        if here:
            act_exp(act, b, 0)
        if tail:
            act_tail(act, b - 1)
        if proj and where is FULL:
            act_tr(act, b + 2, at, where)
        if here:
            act_exp(act, b, 1)
            act_cT(act, b, 0)
        if proj and where is FULL:
            act_qk(act, b + 2, at, where)
        if here:
            act_exp(act, b, 2)
            act_cT(act, b, 1)
            act_exp(act, b, 3)
            act_cT(act, b, 2)
        if proj:
            if where is not FULL:
                act_tr(act, b + 2, at, where)
                act_qk(act, b + 2, at, where)
            act_stacks(act, b + 2, par, at, where)
        if here:
            act_cT(act, b, 3)

    def dve_stats(dve, b):
        for j in range(SB):
            last = nc.vector.bn_stats(stats[:, j, :], x[:, ds(b * SEQ + j * P, P)])
        link(dve, s_stat, last)
        for j in range(SB):
            last = nc.vector.bn_aggr(mv[:, j, :], stats[:, j, :])
        link(dve, s_stat, last)
        nc.vector.tensor_scalar_add(veps[:], mv[:, :, 1], EPS).then_inc(s_var, 1)

    def dve_xn(dve, b):
        dve.wait_ge(s_rstd, b + 1)
        for j in range(SB):
            last = nc.vector.tensor_scalar(xn[:, j, :], x[:, ds(b * SEQ + j * P, P)], mv[:, j, 0:1],
                                           rstd[:, j:j + 1], ALU.subtract, ALU.mult)
        last.then_inc(s_xn, 1)

    def dve_qkl(dve, b, at, where):
        dve.wait_ge(s_qkh, b + 1)
        bank, _ = ring(at, where["qk"])
        nc.vector.tensor_tensor(qkl[:].rearrange("p a t -> p (a t)"), b_ring[bank][:, :],
                                qkh[:].rearrange("p a t -> p (a t)"), ALU.subtract).then_inc(s_free[bank], 1)

    def dve_v(dve, b, par, at, where):
        bank = wait_full(dve, at, where["v"])
        for j in range(SB):
            last = nc.vector.tensor_copy(va[par][:, j, :, 0:HD],
                                         b_ring[bank][:, j * P:(j + 1) * P].rearrange("p (h d) -> p h d", d=HD))
        last.then_inc(s_free[bank], 1)

    def dve_max(dve, b, at, where, g):
        for part in range(3):
            bank = wait_full(dve, at, where["max"][g] + part)
            if part == 0:
                o = mx[:, 0, GH * g:GH * g + GH]
                s = b_ring[bank][:, :].rearrange("p (i k) -> p i k", k=P)
            else:
                o = mx[:, 1, GH * g + 2 * part - 2:GH * g + 2 * part]
                s = b_ring[bank][:, :].rearrange("p (i k) -> p i k", k=SEQ)
            nc.vector.reduce_max(o, s, AX.X).then_inc(s_free[bank], 1)

    def dve_m(dve, b, par, at, where):
        for n in (where["max"][3] + 1, where["max"][3] + 2):
            bank, k = ring(at, n)
            dve.wait_ge(s_free[bank], k + 2)
        for j in range(SB):
            last = nc.vector.tensor_scalar(marr[:, j, :, :, SLOT], mx[:, j, :].rearrange("p (r n) -> p n r", n=NG),
                                           -1.0, None, ALU.mult)
        last.then_inc(s_marr, 1)
        for u in range(2):
            bank = wait_full(dve, at, where["m"] + u)
            q = qs[par][:, 2 * u:2 * u + 2, :].rearrange("p g t -> p (g t)")
            nc.vector.tensor_tensor(q, q, b_ring[bank][:, :], ALU.add).then_inc(s_free[bank], 1)

    def dve_norm(dve, b):
        dve.wait_ge(s_ct, b * 4 + (4 + 2))
        for j in range(SB):
            c = b_c[j][:, :].rearrange("p (h r) -> p h r", r=32)
            last = nc.vector.reciprocal(rden[:, j, :], c[:, :, HD])
        last.then_inc(s_rden, 1)
        dve.wait_ge(s_rden, b + 1)
        for j in range(SB):
            c = b_c[j][:, :].rearrange("p (h r) -> p h r", r=32)
            last = nc.vector.tensor_tensor(cn[:, j, :].rearrange("p (n r d) -> p r n d", r=GH, d=HD),
                                           c.rearrange("p (r n) c -> p r n c", n=NG)[:, :, :, 0:HD],
                                           rden[:, j, :].rearrange("p (r n) -> p r n", n=NG).unsqueeze(3)
                                           .to_broadcast([P, GH, NG, HD]), ALU.mult)
        last.then_inc(s_cn, 1)

    def dve_add(dve, b):
        dve.wait_ge(s_o, b + 1)
        xs = x[:, ds(b * SEQ, SEQ)]
        nc.vector.tensor_tensor(xs, b_c[1][:, 0:SEQ], xs, ALU.add).then_inc(s_x, 1)

    def dve_step(dve, b, par, at, where, tail=True, here=True, maxima=True, proj=True):
        if tail:
            dve_norm(dve, b - 1)
        if proj:
            dve_stats(dve, b + 2)
        if maxima:
            dve_max(dve, b + 1, at, where, 0)
        if proj:
            dve_xn(dve, b + 2)
        if maxima:
            dve_max(dve, b + 1, at, where, 1)
        if tail:
            dve_add(dve, b - 1)
        if proj and where is FULL:
            dve_qkl(dve, b + 2, at, where)
        if maxima:
            dve_max(dve, b + 1, at, where, 2)
            dve_max(dve, b + 1, at, where, 3)
            dve_m(dve, b + 1, 1 - par, at, where)
        if proj:
            if where is not FULL:
                dve_qkl(dve, b + 2, at, where)
            dve_v(dve, b + 2, par, at, where)

    def pool_rstd(pool, b):
        take(pool, s_var)
        nc.gpsimd.tensor_tensor(rstd[:], veps[:], neg_half[:, 0:SB], ALU.pow).then_inc(s_rstd, 1)

    def pool_mask(pool, b, g):
        for part in range(3):
            take(pool, s_e[part])
            n, w = (4, P) if part == 2 else (2, SEQ)
            v = pt[g % 2][:, part, :].rearrange("p (i q) -> p i q", q=w)[:, :, 0:P]
            nc.gpsimd.affine_select(out=v, in_=v, compare_op=ALU.is_ge, fill=0.0, base=0,
                                    pattern=[[0, n], [1, P]], channel_multiplier=-1).then_inc(s_p[part], 1)

    LOOP = NB - 2

    with nc.Block() as block:
        @block.tensor
        def _(pe):
            pe.sem_inc(s_pv, 2)
            pe.sem_inc(s_ct, 2)
            pe.wait_ge(s_const, 1)
            pe_step(pe, -2, 0, (0, 0), FIRST, tail=False, here=False, maxima=False)
            pe_step(pe, -1, 1, (0, START - PER), FULL, tail=False, here=False)
            pe_step(pe, 0, 0, (0, START), FULL, tail=False)
            pe_step(pe, 1, 1, (0, START + PER), FULL)
            with pe.Fori(1, LOOP // 2) as pair:
                pe_step(pe, pair * 2, 0, (pair * PER, START), FULL)
                pe_step(pe, pair * 2 + 1, 1, (pair * PER, START + PER), FULL)
            pe_step(pe, NB - 2, 0, (0, START + PER * (NB - 2)), LEAN, proj=False)
            pe_step(pe, NB - 1, 1, (0, START + PER * (NB - 1)), LEAN, maxima=False, proj=False,
                    m_back=LEAN["m"] - PER)
            pe_tail_a(pe, NB - 1)
            pe_tail_b(pe, NB - 1)

        @block.scalar
        def _(act):
            act.sem_inc(s_cT, 1)
            act.wait_ge(s_const, 1)
            act_step(act, -2, 0, (0, 0), FIRST, tail=False, here=False, maxima=False)
            act_step(act, -1, 1, (0, START - PER), FULL, tail=False, here=False)
            act_step(act, 0, 0, (0, START), FULL, tail=False)
            act_step(act, 1, 1, (0, START + PER), FULL)
            with act.Fori(1, LOOP // 2) as pair:
                act_step(act, pair * 2, 0, (pair * PER, START), FULL)
                act_step(act, pair * 2 + 1, 1, (pair * PER, START + PER), FULL)
            act_step(act, NB - 2, 0, (0, START + PER * (NB - 2)), LEAN, proj=False)
            act_step(act, NB - 1, 1, (0, 0), LEAN, maxima=False, proj=False)
            act_tail(act, NB - 1)

        @block.vector
        def _(dve):
            for s in s_free + [s_x]:
                dve.sem_inc(s, 1)
            nc.vector.memset(marr[:], 0.0)
            for i in range(2):
                nc.vector.memset(va[i][:], 0.0)
            for k in sel:
                last = nc.vector.memset(sel[k][:], 0.0)
            last.then_inc(s_zero, 1)
            dve.wait_ge(s_zero, 1)
            for i in range(2):
                nc.vector.memset(va[i][:, :, :, HD:HD + 1], 1.0)
            for k, slots in SLOTS.items():
                for g in range(NG):
                    for s in slots:
                        nc.vector.tensor_copy(sel[k][:, g, :, s, :],
                                              ident_h[:, 32 * g:32 * g + 32].rearrange("p (i d) -> p i d", d=HD))
            nc.vector.reduce_sum(kones[:], ident[:].rearrange("p (i r) -> p i r", r=32)[:, :, SLOT],
                                 AX.X).then_inc(s_const, 1)
            dve_step(dve, -2, 0, (0, 0), FIRST, tail=False, here=False, maxima=False)
            dve_step(dve, -1, 1, (0, START - PER), FULL, tail=False, here=False)
            dve_step(dve, 0, 0, (0, START), FULL, tail=False)
            dve_step(dve, 1, 1, (0, START + PER), FULL)
            with dve.Fori(1, LOOP // 2) as pair:
                dve_step(dve, pair * 2, 0, (pair * PER, START), FULL)
                dve_step(dve, pair * 2 + 1, 1, (pair * PER, START + PER), FULL)
            dve_step(dve, NB - 2, 0, (0, START + PER * (NB - 2)), LEAN, proj=False)
            dve_step(dve, NB - 1, 1, (0, 0), LEAN, maxima=False, proj=False)
            dve_norm(dve, NB - 1)
            dve_add(dve, NB - 1)

        @block.gpsimd
        def _(pool):
            for s in s_p:
                pool.sem_inc(s, 1)
            pool_rstd(pool, 0)
            pool_rstd(pool, 1)
            with pool.Fori(0, LOOP) as b:
                pool_mask(pool, b, 0)
                pool_rstd(pool, b + 2)
                for g in range(1, NG):
                    pool_mask(pool, b, g)
            for b in (NB - 2, NB - 1):
                for g in range(NG):
                    pool_mask(pool, b, g)


_INS = ['L0_attn_x', 'L0_attn_q_proj', 'L0_attn_k_proj', 'L0_attn_v_proj', 'L0_attn_out_proj', 'L0_ffn_gate_W',
        'L0_ffn_W1', 'L0_ffn_b1', 'L0_ffn_W2', 'L0_ffn_b2']
_OUTS = [((32, 256, 128), 'float32')]


def kernel(**inputs):
    import numpy as _np
    import concourse.bacc as _bacc
    from concourse import mybir as _mybir
    from concourse.bass_utils import run_bass_kernel_spmd as _run

    nc = _bacc.Bacc("TRN2", target_bir_lowering=False, num_devices=1)
    arrays, args = {}, []
    for name in _INS:
        a = _np.ascontiguousarray(inputs[name])
        arrays[f"in_{name}_dram"] = a
        args.append(nc.dram_tensor(f"in_{name}_dram", a.shape, _mybir.dt.from_np(a.dtype), kind="ExternalInput").ap())
    for i, (shape, dtype) in enumerate(_OUTS):
        dt = _mybir.dt.from_np(_np.dtype(dtype))
        args.append(nc.dram_tensor(f"out_{i}_dram", shape, dt, kind="ExternalOutput").ap())
    build(nc, *args)
    r = _run(nc, [arrays], core_ids=[0])
    return r.results[0]["out_0_dram"]
```

```python
import concourse.bass as bass
from concourse import mybir
from contextlib import ExitStack


fp32 = mybir.dt.float32
fp16 = mybir.dt.float16
bf16 = mybir.dt.bfloat16
ALU = mybir.AluOpType
ACT = mybir.ActivationFunctionType
AX = mybir.AxisListType

P = 128
NB, SEQ, D = 32, 256, 128
SB = SEQ // P
NBLK = NB * SB
E, HID = 8, 256
HC = HID // P
TB = 4
TT = TB * P
NT = NBLK // TB
H, HD = 16, 8
NG, NR = 4, 4
SLOT = 3 * HD
EPS = 1e-5
SCALE = 1.0 / float(HD) ** 0.5
WS = 8.0
BIG = -1.0e30


def ds(start, size):
    return bass.ds(start, size)


class Step:

    def __init__(self, b, par, cur, nxt, load, tail=True, here=True, maxima=True, proj=True, settle=False,
                 second=False, first_of_loop=False, opening=0):
        self.b, self.par, self.cur, self.nxt, self.load = b, par, cur, nxt, load
        self.tail, self.here, self.maxima, self.proj, self.settle = tail, here, maxima, proj, settle
        self.alone = not (here or maxima)
        self.second, self.first_of_loop, self.opening = second, first_of_loop, opening


def fixed_steps(i):
    out = []
    for b in (2 * i, 2 * i + 1):
        even = b % 2 == 0
        cur, nxt = (i + 2, i - 1) if even else (i - 1, i + 3)
        out.append(Step(b, b % 2, cur if 0 <= cur < NT else None, nxt if 0 <= nxt < NT else None, not even,
                        tail=1 <= b <= NB, here=0 <= b < NB, maxima=-1 <= b < NB - 1, proj=-2 <= b < NB - 2,
                        settle=b >= NB - 1, second=not even))
    return out


def loop_steps(i):
    return [Step(i * 2, 0, i + 2, i - 1, False, first_of_loop=True),
            Step(i * 2 + 1, 1, i - 1, i + 3, True, second=True)]


def run_all(eng, step):
    none = dict(tail=False, here=False, maxima=False, proj=False)
    step(Step(-4, 0, None, 0, True, opening=1, **none))
    step(Step(-3, 1, 0, 1, True, opening=2, **none))
    for i in range(-1, 1):
        for st in fixed_steps(i):
            step(st)
    with eng.Fori(1, NT - 3) as i:
        for st in loop_steps(i):
            step(st)
    for i in range(NT - 3, NT + 1):
        for st in fixed_steps(i):
            step(st)


def build(nc, x_in, q_proj, k_proj, v_proj, out_proj, gate_w, w1_in, b1_in, w2_in, b2_in, out):
    xin_v = x_in.rearrange("b (k p) d -> p (b k) d", p=P)
    out_v = out.rearrange("b (k p) d -> p (b k) d", p=P)
    ctx = ExitStack()
    with ctx:
        def sb(name, shape, dt):
            return ctx.enter_context(nc.sbuf_tensor(name, shape, dt))

        def sem(name):
            return ctx.enter_context(nc.semaphore(name))

        x = sb("x", [P, NBLK * D], fp32)
        ident = sb("ident", [P, P], fp32)
        ident_h = sb("ident_h", [P, P], fp16)
        ident_b = sb("ident_b", [P, P], bf16)
        gw = sb("gw", [P, E], fp32)
        w1f = sb("w1f", [P, E * HID], fp32)
        w1 = [sb(f"w1_{k}", [P, E * HID], fp16) for k in ("hi", "lo")]
        w2f = sb("w2f", [P, E * HC * D], fp32)
        w2 = [sb(f"w2_{k}", [P, E * HC * D], fp16) for k in ("hi", "lo")]
        b1r = sb("b1r", [E * HC, P], fp32)
        b1 = sb("b1", [P, E * HC], fp32)
        b2f = sb("b2f", [96, D], fp32)
        b2 = sb("b2", [96, D], fp16)
        wq, wk, wv, wo = (sb(n, [P, D], fp32) for n in ("wq", "wk", "wv", "wo"))
        mask = sb("mask", [P, NG, P], bf16)
        neg_half = sb("neg_half", [P, TB], fp32)
        order = sb("order", [P, TB, E], fp32)
        sel = {k: sb(f"sel_{k}", [P, NG, NR, 4, HD], fp16) for k in ("qh", "ql", "kh", "kl")}
        SLOTS = {"qh": (0, 1), "ql": (2,), "kh": (0, 2), "kl": (1,)}
        kones = sb("kones", [P, 1], fp32)

        stats = sb("stats", [P, TB, 6], fp32)
        mv = sb("mv", [P, TB, 2], fp32)
        veps = sb("veps", [P, TB], fp32)
        rstd = sb("rstd", [P, TB], fp32)
        xn = sb("xn", [P, TB, D], fp32)
        xT = sb("xT", [P, TT], fp32)
        xTh = [sb(f"xTh{i}", [P, TT], fp16) for i in range(2)]
        xTl = [sb(f"xTl{i}", [P, TT], fp16) for i in range(2)]
        small = sb("small", [P, 9, TB], fp32)
        wide = sb("wide", [P, 10, TB, E], fp32)
        cw = [sb(f"cw{i}", [P, TB, E], fp32) for i in range(2)]
        half = sb("half", [P, TB, E], fp32)
        cw3 = sb("cw3", [P, TB, 3, 32], fp16)
        cwT = sb("cwT", [96, TT], fp16)
        hf = [sb(f"hf{i}", [P, HC, TT], fp32) for i in range(2)]
        hh = [sb(f"hh{i}", [P, HC, TT], fp16) for i in range(2)]
        hl = [sb(f"hl{i}", [P, HC, TT], fp16) for i in range(2)]
        spare = sb("spare", [P, 4], fp32)

        a_stats = sb("a_stats", [P, SB, 6], fp32)
        a_mv = sb("a_mv", [P, SB, 2], fp32)
        a_veps = sb("a_veps", [P, SB], fp32)
        a_rstd = sb("a_rstd", [P, SB], fp32)
        a_xn = sb("a_xn", [P, SB, D], fp32)
        a_xT = sb("a_xT", [P, SEQ], fp32)
        qkh = sb("qkh", [P, 2, SEQ], fp16)
        qkl = sb("qkl", [P, 2, SEQ], fp16)
        qs = [sb(f"qs{i}", [P, NG, SEQ], fp16) for i in range(2)]
        ks = [sb(f"ks{i}", [P, NG, SEQ], fp16) for i in range(2)]
        va = [sb(f"va{i}", [P, SB, H, 32], fp32) for i in range(2)]
        mx = sb("mx", [P, SB, NR * NG], fp32)
        marr = sb("marr", [P, SB, NG, NR, 4 * HD], fp16)
        pt = [sb(f"pt{i}", [P, 3, 512], fp32) for i in range(2)]
        cT = sb("cT", [P, SEQ], fp32)
        rden = sb("rden", [P, SB, NG], fp32)
        cn = sb("cn", [P, SB, D], fp32)
        cnT = sb("cnT", [P, SEQ], fp32)

        ps = [ctx.enter_context(nc.psum_tensor(f"bank{i}", [P, 512], fp32)) for i in range(8)]
        b_z, b_y, b_ring, b_s, b_pv = ps[0:2], ps[2], ps[3:5], ps[5:7], ps[7]

        s_xin = sem("x_loaded")
        s_store = sem("x_final")
        s_out = sem("x_stored")
        s_var = sem("var")
        s_rstd = sem("rstd")
        s_xn = sem("xn")
        s_xTh = sem("xTh")
        s_shift = sem("shift")
        s_exp = sem("exp")
        s_cw = sem("cw")
        s_z = sem("z")
        s_hf = [sem(f"hf{c}") for c in range(HC)]
        s_hfd = sem("hfd")
        s_h = [sem(f"h{c}") for c in range(HC)]
        s_y = sem("y")
        s_acc = sem("acc")
        s_avar = sem("a_var")
        s_arstd = sem("a_rstd")
        s_axn = sem("a_xn")
        s_ring_a = sem("ring_a")
        s_ring_d = sem("ring_d")
        s_free = [sem(f"free{i}") for i in range(2)]
        s_qkh = sem("qkh")
        s_marr = sem("marr")
        s_s = sem("s")
        s_e = sem("e")
        s_p = sem("p")
        s_pv = sem("pv")
        s_cT = sem("cT")
        s_ct = sem("ct")
        s_cn = sem("cn")
        s_dve = sem("dve")
        s_x = sem("x")
        s_norm = sem("norm")
        s_anorm = sem("a_norm")
        s_gate = sem("gate")
        s_div = sem("div")

        w_in = [sem(f"w_in{i}") for i in range(4)]
        s_zero, s_ident, s_b1 = sem("zero"), sem("ident"), sem("b1_t")
        s_wh = [sem(f"w{n + 1}_high") for n in range(2)]
        s_wl = [sem(f"w{n + 1}_low") for n in range(2)]
        s_izero, s_own = sem("ident_zero"), sem("b2_high")

        with nc.Block() as block:
            @block.sync
            def _(sp):
                sp.dma_start(x[:, 0:TT].rearrange("p (k d) -> p k d", d=D), xin_v[:, 0:TB, :]).then_inc(s_xin, 16)
                for dst, src in ((b1r, b1_in.rearrange("e (c p) -> (e c) p", p=P)), (gw, gate_w)):
                    sp.dma_start(dst[:], src).then_inc(w_in[2], 16)
                sp.dma_start(w1f[:].rearrange("d (e h) -> d e h", e=E),
                             w1_in.rearrange("e d h -> d e h")).then_inc(w_in[0], 16)
                sp.wait_ge(s_zero, 1)
                for k in range(3):
                    sp.dma_start(b2f[32 * k:32 * k + E, :], b2_in).then_inc(w_in[2], 16)
                sp.dma_start(w2f[:].rearrange("p (n o) -> p n o", o=D),
                             w2_in.rearrange("e (c p) o -> p (e c) o", p=P)).then_inc(w_in[1], 16)
                for dst, src in ((wq, q_proj), (wk, k_proj), (wv, v_proj), (wo, out_proj)):
                    sp.dma_start(dst[:], src).then_inc(w_in[3], 16)
                sp.wait_ge(s_xin, 16)
                sp.wait_ge(w_in[2], 80)

            @block.gpsimd
            def _(pool):
                nc.gpsimd.memset(ident[:], 0.0)
                nc.gpsimd.memset(mask[:], 0.0).then_inc(s_izero, 1)
                nc.gpsimd.memset(neg_half[:], -0.5)
                for e in range(E):
                    nc.gpsimd.memset(order[:, :, e], float(E - e))
                pool.wait_ge(s_izero, 1)
                nc.gpsimd.affine_select(out=ident[:], in_=ident[:], compare_op=ALU.not_equal, fill=1.0, base=0,
                                        pattern=[[-1, P]], channel_multiplier=1).then_inc(s_ident, 1)
                nc.gpsimd.affine_select(out=mask[:], in_=mask[:], compare_op=ALU.is_ge, fill=BIG, base=0,
                                        pattern=[[0, NG], [-1, P]], channel_multiplier=1)

            @block.tensor
            def _(pe):
                pe.wait_ge(s_ident, 1)
                pe.wait_ge(w_in[2], 80)
                nc.tensor.transpose(ps[0][:, 0:E * HC], b1r[:], ident[0:E * HC, 0:E * HC]).then_inc(s_b1, 1)

            @block.scalar
            def _(act):
                act.wait_ge(w_in[0], 16)
                nc.scalar.activation(w1[0][:], w1f[:], ACT.Copy, scale=WS).then_inc(s_wh[0], 1)

            @block.vector
            def _(dve):
                nc.vector.memset(b2f[:], 0.0).then_inc(s_zero, 1)
                nc.vector.memset(cw3[:], 0.0)
                nc.vector.memset(marr[:], 0.0)
                for i in range(2):
                    nc.vector.memset(va[i][:], 0.0)
                for k in sel:
                    last = nc.vector.memset(sel[k][:], 0.0)
                last.then_inc(s_own, 1)
                dve.wait_ge(s_own, 1)
                dve.sem_inc(s_own, -1)
                for i in range(2):
                    nc.vector.memset(va[i][:, :, :, HD:HD + 1], 1.0)
                dve.wait_ge(s_ident, 1)
                nc.vector.reduce_sum(kones[:], ident[:].rearrange("p (i r) -> p i r", r=32)[:, :, SLOT], AX.X)
                nc.vector.tensor_copy(ident_b[:], ident[:])
                nc.vector.tensor_copy(ident_h[:], ident[:]).then_inc(s_dve, 1)
                dve.wait_ge(s_dve, 1)
                dve.sem_inc(s_dve, -1)
                for k, slots in SLOTS.items():
                    for g in range(NG):
                        for s in slots:
                            nc.vector.tensor_copy(sel[k][:, g, :, s, :],
                                                  ident_h[:, 32 * g:32 * g + 32].rearrange("p (i d) -> p i d", d=HD))
                dve.wait_ge(s_b1, 1)
                nc.vector.tensor_scalar(b1[:], ps[0][:, 0:E * HC], WS, None, ALU.mult)
                nc.vector.tensor_scalar(b2[:], b2f[:], WS * WS, None, ALU.mult).then_inc(s_own, 1)
                dve.wait_ge(s_own, 1)
                nc.vector.scalar_tensor_tensor(out=b2[64:96, :], in0=b2f[64:96, :], scalar=WS * WS,
                                               in1=b2[64:96, :], op0=ALU.mult, op1=ALU.subtract)

        with nc.Block() as block:
            @block.sync
            def _(sp):
                with sp.Fori(1, NT) as t:
                    sp.wait_ge(s_xin, t * 16)
                    sp.dma_start(x[:, ds(t * TT, TT)].rearrange("p (k d) -> p k d", d=D),
                                 xin_v[:, ds(t * TB, TB), :]).then_inc(s_xin, 16)
                sp.wait_ge(s_store, 1)
                sp.sem_inc(s_store, -1)
                with sp.Fori(0, NT) as t:
                    sp.wait_ge(s_store, 1)
                    sp.sem_inc(s_store, -1)
                    sp.dma_start(out_v[:, ds(t * TB, TB), :],
                                 x[:, ds(t * TT, TT)].rearrange("p (k d) -> p k d", d=D)).then_inc(s_out, 16)
                sp.wait_ge(s_out, NT * 16)

            @block.tensor
            def _(pe):
                def first_product(par, e):
                    for c in range(HC):
                        pe.wait_ge(s_h[c], 1)
                        pe.sem_inc(s_h[c], -1)
                        w = slice(e * HID + c * P, e * HID + (c + 1) * P)
                        nc.tensor.matmul(b_z[c][:, :], w1[0][:, w], xTh[par][:], start=True, stop=False)
                        nc.tensor.matmul(b_z[c][:, :], w1[0][:, w], xTl[par][:], start=False, stop=False)
                        nc.tensor.matmul(b_z[c][:, :], w1[1][:, w], xTh[par][:],
                                         start=False, stop=True).then_inc(s_z, 1)

                def second_product(e, followed, final):
                    if not followed:
                        for c in range(HC):
                            pe.wait_ge(s_h[c], 1)
                    pe.wait_ge(s_acc, 1)
                    pe.sem_inc(s_acc, -1)
                    if final:
                        pe.sem_inc(s_store, 1)
                    for j in range(TB):
                        o, t = b_y[:, j * P:(j + 1) * P], slice(j * P, (j + 1) * P)
                        for c in range(HC):
                            w = slice((e * HC + c) * D, (e * HC + c + 1) * D)
                            nc.tensor.matmul(o, hh[e % 2][:, c, t], w2[0][:, w], start=(c == 0), stop=False)
                            nc.tensor.matmul(o, hh[e % 2][:, c, t], w2[1][:, w], start=False, stop=False)
                            last = nc.tensor.matmul(o, hl[e % 2][:, c, t], w2[0][:, w],
                                                    start=False, stop=(c == HC - 1))
                    last.then_inc(s_y, 1)

                def blocks(bank, n=SB):
                    return [b_ring[bank][:, j * P:(j + 1) * P] for j in range(n)]

                def f_tr():
                    pe.wait_ge(s_xn, 1)
                    pe.sem_inc(s_xn, -1)
                    pe.wait_ge(s_free[1], 1)
                    pe.sem_inc(s_free[1], -1)
                    for j, o in enumerate(blocks(1, TB)):
                        last = nc.tensor.transpose(o, xn[:, j, :], ident[:])
                    last.then_inc(s_ring_a, 1)

                def f_logit():
                    pe.wait_ge(s_free[1], 1)
                    pe.sem_inc(s_free[1], -1)
                    for j in range(TB):
                        last = nc.tensor.matmul(b_ring[1][:, j * E:(j + 1) * E], xT[:, j * P:(j + 1) * P], gw[:],
                                                start=True, stop=True)
                    last.then_inc(s_ring_d, 1)

                def f_cwT():
                    pe.wait_ge(s_cw, 1)
                    pe.sem_inc(s_cw, -1)
                    pe.wait_ge(s_free[1], 1)
                    pe.sem_inc(s_free[1], -1)
                    for j in range(TB):
                        last = nc.tensor.matmul(b_ring[1][0:96, j * P:(j + 1) * P],
                                                cw3[:, j].rearrange("p k e -> p (k e)"), ident_h[:],
                                                start=True, stop=True)
                    last.then_inc(s_ring_a, 1)

                def f_bias():
                    pe.wait_ge(s_free[1], 1)
                    pe.sem_inc(s_free[1], -1)
                    for j, o in enumerate(blocks(1, TB)):
                        last = nc.tensor.matmul(o, cwT[:, j * P:(j + 1) * P], b2[:], start=True, stop=True)
                    last.then_inc(s_ring_d, 1)

                def a_tr():
                    pe.wait_ge(s_axn, 1)
                    pe.sem_inc(s_axn, -1)
                    pe.wait_ge(s_free[1], 1)
                    pe.sem_inc(s_free[1], -1)
                    for j, o in enumerate(blocks(1)):
                        last = nc.tensor.transpose(o, a_xn[:, j, :], ident[:])
                    last.then_inc(s_ring_a, 1)

                def a_qk():
                    pe.wait_ge(s_free[1], 1)
                    pe.sem_inc(s_free[1], -1)
                    for i, w in enumerate((wq, wk)):
                        last = nc.tensor.matmul(b_ring[1][:, i * SEQ:(i + 1) * SEQ], w[:], a_xT[:],
                                                start=True, stop=True)
                    last.then_inc(s_ring_a, 1)

                def a_stack(u):
                    bank, i, half = 1 - u % 2, u % 2, u // 2
                    pe.wait_ge(s_free[bank], 1)
                    pe.sem_inc(s_free[bank], -1)
                    for g in range(2):
                        o = b_ring[bank][:, g * SEQ:(g + 1) * SEQ]
                        hi, lo = (sel[k][:, 2 * half + g].rearrange("p i s d -> p (i s d)")
                                  for k in (("qh", "ql"), ("kh", "kl"))[i])
                        nc.tensor.matmul(o, hi, qkh[:, i, :], start=True, stop=False)
                        last = nc.tensor.matmul(o, lo, qkl[:, i, :], start=False, stop=True)
                    last.then_inc(s_ring_a, 1)

                def a_v():
                    pe.wait_ge(s_free[1], 1)
                    pe.sem_inc(s_free[1], -1)
                    for j, o in enumerate(blocks(1)):
                        last = nc.tensor.matmul(o, a_xT[:, j * P:(j + 1) * P], wv[:], start=True, stop=True)
                    last.then_inc(s_ring_a, 1)

                def a_max(par, r, part, bank):
                    pe.wait_ge(s_free[bank], 1)
                    pe.sem_inc(s_free[bank], -1)
                    rows = slice(32 * r, 32 * r + 32)
                    o = b_ring[bank]
                    for n, g in enumerate(range(NG) if part == 0 else (2 * part - 2, 2 * part - 1)):
                        if part == 0:
                            nc.tensor.matmul(o[:, n * P:(n + 1) * P], qs[par][rows, g, 0:P], ks[par][rows, g, 0:P],
                                             start=True, stop=False, tile_position=(32 * r, 0),
                                             skip_group_check=True)
                        else:
                            nc.tensor.matmul(o[:, n * SEQ:(n + 1) * SEQ], qs[par][rows, g, P:SEQ],
                                             ks[par][rows, g, :], start=True, stop=False,
                                             tile_position=(32 * r, 0), skip_group_check=True)
                    if part == 0:
                        o, m = o[:, :], mask[:].rearrange("p i k -> p (i k)")
                    else:
                        o, m = o[:, :].rearrange("p (i k) -> p i k", k=SEQ)[:, :, P:SEQ], mask[:, 0:2, :]
                    nc.tensor.matmul(o, ident_b[:], m, start=False, stop=True,
                                     skip_group_check=True).then_inc(s_ring_d, 1)

                def a_m(u):
                    if u == 0:
                        pe.wait_ge(s_marr, 1)
                        pe.sem_inc(s_marr, -1)
                    pe.wait_ge(s_free[u], 1)
                    pe.sem_inc(s_free[u], -1)
                    for g in range(2):
                        for j in range(SB):
                            o = b_ring[u][:, g * SEQ + j * P:g * SEQ + (j + 1) * P]
                            last = nc.tensor.matmul(o, marr[:, j, 2 * u + g].rearrange("p i r -> p (i r)"),
                                                    ident_h[:], start=True, stop=True)
                    last.then_inc(s_ring_d, 1)

                def a_scores(par, r, part):
                    pe.wait_ge(s_p, 1)
                    pe.sem_inc(s_p, -1)
                    rows = slice(32 * r, 32 * r + 32)
                    bank = b_s[(3 * r + part) % 2]
                    for n, g in enumerate(range(NG) if part == 2 else (2 * part, 2 * part + 1)):
                        if part == 2:
                            last = nc.tensor.matmul(bank[:, n * P:(n + 1) * P], ks[par][rows, g, P:SEQ],
                                                    qs[par][rows, g, P:SEQ], start=True, stop=True,
                                                    tile_position=(32 * r, 0))
                        else:
                            last = nc.tensor.matmul(bank[:, n * SEQ:(n + 1) * SEQ], ks[par][rows, g, 0:P],
                                                    qs[par][rows, g, :], start=True, stop=True,
                                                    tile_position=(32 * r, 0))
                    last.then_inc(s_s, 1)

                def a_pv(par, r):
                    pe.wait_ge(s_p, 2)
                    pe.wait_ge(s_cn, 1)
                    pe.sem_inc(s_cn, -1)
                    for g in range(NG):
                        nc.tensor.matmul(b_pv[32 * g:32 * g + 32, 0:SEQ], va[par][:, 0, NR * g + r, :],
                                         pt[r % 2][:, g // 2, (g % 2) * SEQ:(g % 2 + 1) * SEQ],
                                         start=True, stop=False, tile_position=(0, 32 * g), skip_group_check=True)
                    for g in range(NG):
                        last = nc.tensor.matmul(b_pv[32 * g:32 * g + 32, P:SEQ], va[par][:, 1, NR * g + r, :],
                                                pt[r % 2][:, 2, g * P:(g + 1) * P], start=False, stop=True,
                                                tile_position=(0, 32 * g), skip_group_check=True)
                    last.then_inc(s_pv, 1)

                def a_ct():
                    pe.wait_ge(s_cT, 1)
                    pe.sem_inc(s_cT, -1)
                    for j in range(SB):
                        last = nc.tensor.transpose(b_pv[:, SEQ + j * P:SEQ + (j + 1) * P],
                                                   cT[:, j * P:(j + 1) * P], ident[:])
                    last.then_inc(s_ct, 1)

                def a_tail_a():
                    pe.wait_ge(s_cn, 1)
                    pe.wait_ge(s_free[1], 1)
                    pe.sem_inc(s_free[1], -1)
                    for j, o in enumerate(blocks(1)):
                        last = nc.tensor.transpose(o, cn[:, j, :], ident[:])
                    last.then_inc(s_ring_a, 1)

                def a_tail_b():
                    pe.wait_ge(s_free[1], 1)
                    pe.sem_inc(s_free[1], -1)
                    for j, o in enumerate(blocks(1)):
                        last = nc.tensor.matmul(o, cnT[:, j * P:(j + 1) * P], wo[:], start=True, stop=True)
                    last.then_inc(s_ring_d, 1)

                def ahead(st, s):
                    if s == 0 and st.here and st.settle:
                        for k in range(2):
                            pe.wait_ge(s_free[k], 1)
                    if s % 2 == 0 and st.here:
                        a_scores(st.par, s // 2, 0)
                        a_scores(st.par, s // 2, 1)
                    if s == 6 and st.cur is not None:
                        f_bias()

                def between(st, s):
                    m, other = st.maxima, 1 - st.par
                    if s % 2 == 0 and (st.here if s else st.tail):
                        a_ct()
                    if s == 0:
                        if m:
                            a_max(other, 0, 2, 0)
                    if s == 1:
                        if m:
                            a_max(other, 0, 1, 0)
                        if st.tail:
                            a_tail_b()
                    if s == 2:
                        if m:
                            a_max(other, 1, 2, 0)
                        if st.proj:
                            a_tr()
                    if s == 3:
                        if m:
                            a_max(other, 2, 2, 0)
                        if st.proj:
                            a_qk()
                    if s == 4:
                        if m:
                            a_max(other, 3, 1, 0)
                        if st.nxt is not None:
                            f_logit()
                    if s == 5 and st.cur is not None:
                        f_cwT()
                    if s == 6 and m:
                        a_m(1)
                    if s == 7 and st.proj:
                        a_stack(2)
                        a_stack(3)

                def behind(st, s):
                    par, m, other = st.par, st.maxima, 1 - st.par
                    if s % 2 == 0 and st.here:
                        a_scores(par, s // 2, 2)
                    if s % 2 == 1 and st.here:
                        a_pv(par, s // 2)
                    if s == 3 and st.nxt is not None:
                        f_tr()
                    if s == 0:
                        if m:
                            a_max(other, 0, 0, 0)
                        if st.tail:
                            a_tail_a()
                    if s in (1, 2) and m:
                        a_max(other, s, 0, 0)
                        a_max(other, s, 1, 1)
                    if s == 3 and m:
                        a_max(other, 3, 0, 0)
                    if s == 4 and m:
                        a_max(other, 3, 2, 0)
                    if s == 5 and m:
                        a_m(0)
                    if s == 6 and st.proj:
                        a_stack(0)
                        a_stack(1)
                    if s == 7 and st.proj:
                        a_v()

                state = {"second": False}

                def step(st):
                    for s in range(E):
                        ahead(st, s)
                        if st.cur is not None and s < E - 1:
                            first_product(st.par, s + 1)
                        if s == E - 1 and st.opening == 1:
                            pe.wait_ge(s_wl[0], 1)
                        if s == 0 and st.opening == 2:
                            pe.wait_ge(s_wl[1], 1)
                            pe.wait_ge(w_in[3], 64)
                        if st.nxt is not None and s == E - 1:
                            first_product(1 - st.par, 0)
                        between(st, s)
                        if st.cur is not None:
                            second_product(s, s < E - 1 or st.nxt is not None,
                                           s == 0 and (state["second"] or st.first_of_loop))
                            state["second"] = s == E - 1 and st.second
                        behind(st, s)

                run_all(pe, step)
                pe.wait_ge(s_acc, 1)
                pe.sem_inc(s_acc, -1)
                pe.sem_inc(s_store, 1)

            @block.scalar
            def _(act):
                def relu(par, e, done):
                    for c in range(HC):
                        act.wait_ge(s_z, 1)
                        act.sem_inc(s_z, -1)
                        b = b1[:, e * HC + c:e * HC + c + 1]
                        nc.scalar.activation(hh[par][:, c, :], b_z[c][:, :], ACT.Relu, bias=b)
                        nc.scalar.activation(hf[par][:, c, :], b_z[c][:, :], ACT.Relu, bias=b).then_inc(done[c], 1)

                def exp(r, part):
                    act.wait_ge(s_s, 1)
                    act.sem_inc(s_s, -1)
                    nc.scalar.activation(pt[r % 2][:, part, :], b_s[(3 * r + part) % 2][:, :], ACT.Exp,
                                         scale=SCALE).then_inc(s_e, 1)

                def contexts():
                    act.wait_ge(s_pv, 1)
                    act.sem_inc(s_pv, -1)
                    nc.scalar.copy(cT[:], b_pv[:, 0:SEQ]).then_inc(s_cT, 1)

                def stack(par, u):
                    act.wait_ge(s_ring_a, 1)
                    act.sem_inc(s_ring_a, -1)
                    bank, half = 1 - u % 2, u // 2
                    if u % 2 == 0:
                        nc.scalar.copy(qs[par][:, 2 * half:2 * half + 2, :].rearrange("p g t -> p (g t)"),
                                       b_ring[bank][:, :]).then_inc(s_free[bank], 1)
                    else:
                        nc.scalar.activation(ks[par][:, 2 * half:2 * half + 2, :].rearrange("p g t -> p (g t)"),
                                             b_ring[bank][:, :], ACT.Identity,
                                             bias=kones[:, 0:1]).then_inc(s_free[bank], 1)

                def step(st):
                    for s in range(E):
                        if s % 2 == 0 and (st.here if s else st.tail):
                            contexts()
                        if s % 2 == 0 and st.here:
                            exp(s // 2, 0)
                        if st.cur is not None and s < E - 1:
                            relu((s + 1) % 2, s + 1, (s_hf[0], s_hfd) if st.alone else s_hf)
                        if st.nxt is not None and s == E - 1:
                            relu(0, 0, s_hf)
                        if s % 2 == 0 and st.here:
                            exp(s // 2, 1)
                        if s == 2 and st.proj:
                            act.wait_ge(s_ring_a, 1)
                            act.sem_inc(s_ring_a, -1)
                            nc.scalar.copy(a_xT[:], b_ring[1][:, 0:SEQ]).then_inc(s_free[1], 1)
                        if s == 3 and st.proj:
                            act.wait_ge(s_ring_a, 1)
                            act.sem_inc(s_ring_a, -1)
                            nc.scalar.copy(qkh[:].rearrange("p a t -> p (a t)"), b_ring[1][:, :]).then_inc(s_qkh, 1)
                        if s == 5 and st.cur is not None:
                            act.wait_ge(s_ring_a, 1)
                            act.sem_inc(s_ring_a, -1)
                            nc.scalar.copy(cwT[:], b_ring[1][0:96, :]).then_inc(s_free[1], 1)
                        if s == 7 and st.proj:
                            stack(st.par, 2)
                            stack(st.par, 3)
                        if s % 2 == 0 and st.here:
                            exp(s // 2, 2)
                        if s == 0 and st.tail:
                            act.wait_ge(s_ring_a, 1)
                            act.sem_inc(s_ring_a, -1)
                            nc.scalar.copy(cnT[:], b_ring[1][:, 0:SEQ]).then_inc(s_free[1], 1)
                        if s == 3 and st.nxt is not None:
                            act.wait_ge(s_ring_a, 1)
                            act.sem_inc(s_ring_a, -1)
                            nc.scalar.copy(xT[:], b_ring[1][:, :])
                            nc.scalar.copy(xTh[1 - st.par][:], b_ring[1][:, :]).then_inc(s_xTh, 1)
                        if s == 3 and st.opening == 1:
                            act.wait_ge(w_in[1], 16)
                            nc.scalar.activation(w2[0][:], w2f[:], ACT.Copy, scale=WS).then_inc(s_wh[1], 1)
                        if s == 4 and st.nxt is not None:
                            act.wait_ge(s_shift, 1)
                            act.sem_inc(s_shift, -1)
                            nc.scalar.activation(wide[:, 1], wide[:, 0], ACT.Exp).then_inc(s_exp, 1)
                        if s == 6 and st.proj:
                            stack(st.par, 0)
                            stack(st.par, 1)
                        if s == 7 and st.proj:
                            act.wait_ge(s_ring_a, 1)
                            act.sem_inc(s_ring_a, -1)
                            for j in range(SB):
                                last = nc.scalar.copy(va[st.par][:, j, :, 0:HD],
                                                      b_ring[1][:, j * P:(j + 1) * P].rearrange(
                                                          "p (h d) -> p h d", d=HD))
                            last.then_inc(s_free[1], 1)

                run_all(act, step)

            @block.vector
            def _(dve):
                def mark():
                    nc.vector.memset(spare[:, 0:1], 0.0).then_inc(s_x, 1)

                def norm_stats(base, n, st_, s):
                    dve.wait_ge(s_x, 1)
                    for j in range(n):
                        last = nc.vector.bn_stats(st_[:, j, :], x[:, ds(base + j * P, P)])
                    last.then_inc(s, 1)

                def norm_aggr(n, st_, mv_, s):
                    dve.wait_ge(s, 1)
                    dve.sem_inc(s, -1)
                    for j in range(n):
                        last = nc.vector.bn_aggr(mv_[:, j, :], st_[:, j, :])
                    last.then_inc(s, 1)

                def norm_var(mv_, veps_, s, s_out_):
                    dve.wait_ge(s, 1)
                    dve.sem_inc(s, -1)
                    nc.vector.tensor_scalar_add(veps_[:], mv_[:, :, 1], EPS).then_inc(s_out_, 1)

                def norm_apply(base, n, mv_, rstd_, out_, s_in, s):
                    dve.wait_ge(s_in, 1)
                    dve.sem_inc(s_in, -1)
                    for j in range(n):
                        last = nc.vector.tensor_scalar(out_[:, j, :], x[:, ds(base + j * P, P)], mv_[:, j, 0:1],
                                                       rstd_[:, j:j + 1], ALU.subtract, ALU.mult)
                    last.then_inc(s, 1)

                def split_h(par):
                    dve.wait_ge(s_hfd, 1)
                    dve.sem_inc(s_hfd, -1)
                    nc.vector.tensor_tensor(hl[par][:, 1, :], hf[par][:, 1, :], hh[par][:, 1, :],
                                            ALU.subtract).then_inc(s_h[1], 1)

                def weigh(t, par, e):
                    dve.wait_ge(s_y, 1)
                    dve.sem_inc(s_y, -1)
                    dve.wait_ge(s_x, 1)
                    dve.sem_inc(s_x, -1)
                    for j in range(TB):
                        xs = x[:, ds(t * TT + j * P, P)]
                        last = nc.vector.scalar_tensor_tensor(out=xs, in0=b_y[:, j * P:(j + 1) * P],
                                                              scalar=cw[par][:, j, e:e + 1], in1=xs,
                                                              op0=ALU.mult, op1=ALU.add)
                    last.then_inc(s_acc, 1)
                    mark()

                S, W = small, wide

                def row(i):
                    return S[:, i, :]

                def over(i):
                    return S[:, i, :].unsqueeze(2).to_broadcast([P, TB, E])

                LG = b_ring[1][:, 0:TB * E].rearrange("p (j e) -> p j e", e=E)

                def gate_max():
                    dve.wait_ge(s_ring_d, 1)
                    dve.sem_inc(s_ring_d, -1)
                    nc.vector.reduce_max(row(0), LG, AX.X).then_inc(s_gate, 1)

                def gate_shift():
                    dve.wait_ge(s_gate, 1)
                    dve.sem_inc(s_gate, -1)
                    nc.vector.tensor_tensor(W[:, 0], LG, over(0), ALU.subtract).then_inc(s_shift, 1)
                    nc.vector.memset(spare[:, 3:4], 0.0).then_inc(s_free[1], 1)

                def gate_sum():
                    dve.wait_ge(s_exp, 1)
                    dve.sem_inc(s_exp, -1)
                    nc.vector.reduce_sum(row(1), W[:, 1], AX.X).then_inc(s_gate, 1)

                def gate_inverse():
                    dve.wait_ge(s_gate, 1)
                    dve.sem_inc(s_gate, -1)
                    nc.vector.reciprocal(row(2), row(1)).then_inc(s_gate, 1)

                def gate_probs():
                    dve.wait_ge(s_gate, 1)
                    dve.sem_inc(s_gate, -1)
                    nc.vector.tensor_tensor(W[:, 2], W[:, 1], over(2), ALU.mult).then_inc(s_gate, 1)

                def largest(src, top):
                    dve.wait_ge(s_gate, 1)
                    dve.sem_inc(s_gate, -1)
                    nc.vector.reduce_max(row(top), W[:, src], AX.X).then_inc(s_gate, 1)

                def equals(src, top, equal):
                    dve.wait_ge(s_gate, 1)
                    dve.sem_inc(s_gate, -1)
                    nc.vector.tensor_tensor(W[:, equal], W[:, src], over(top), ALU.is_equal).then_inc(s_gate, 1)

                def ranks(equal, rank):
                    dve.wait_ge(s_gate, 1)
                    dve.sem_inc(s_gate, -1)
                    nc.vector.tensor_tensor(W[:, rank], W[:, equal], order[:], ALU.mult).then_inc(s_gate, 1)

                def gate_rest():
                    dve.wait_ge(s_gate, 1)
                    dve.sem_inc(s_gate, -1)
                    nc.vector.scalar_tensor_tensor(out=W[:, 6], in0=W[:, 5], scalar=-2.0, in1=W[:, 2],
                                                   op0=ALU.mult, op1=ALU.add).then_inc(s_gate, 1)

                def gate_total():
                    dve.wait_ge(s_gate, 1)
                    dve.sem_inc(s_gate, -1)
                    nc.vector.scalar_tensor_tensor(out=row(7), in0=row(3), scalar=1e-8, in1=row(5),
                                                   op0=ALU.add, op1=ALU.add)
                    nc.vector.tensor_tensor(W[:, 3], W[:, 5], W[:, 9], ALU.add).then_inc(s_gate, 1)

                def gate_keep():
                    dve.wait_ge(s_gate, 1)
                    dve.sem_inc(s_gate, -1)
                    nc.vector.reciprocal(row(8), row(7))
                    nc.vector.tensor_tensor(W[:, 4], W[:, 2], W[:, 3], ALU.mult).then_inc(s_gate, 1)

                def gate_half():
                    dve.wait_ge(s_gate, 1)
                    dve.sem_inc(s_gate, -1)
                    nc.vector.scalar_tensor_tensor(out=half[:], in0=W[:, 4], scalar=0.5, in1=over(8),
                                                   op0=ALU.mult, op1=ALU.mult).then_inc(s_gate, 1)

                def gate_parts(par):
                    dve.wait_ge(s_gate, 1)
                    dve.sem_inc(s_gate, -1)
                    nc.vector.tensor_copy(cw3[:, :, 0, 0:E], half[:])
                    nc.vector.tensor_copy(cw3[:, :, 2, 0:E], half[:])
                    nc.vector.tensor_scalar(cw[par][:], half[:], 1.0 / (WS * WS), None,
                                            ALU.mult).then_inc(s_gate, 1)

                def gate_low():
                    dve.wait_ge(s_gate, 1)
                    dve.sem_inc(s_gate, -1)
                    nc.vector.tensor_tensor(cw3[:, :, 1, 0:E], half[:], cw3[:, :, 0, 0:E],
                                            ALU.subtract).then_inc(s_cw, 1)

                def f_init(t):
                    dve.wait_ge(s_x, 1)
                    dve.sem_inc(s_x, -1)
                    xs = x[:, ds(t * TT, TT)]
                    nc.vector.scalar_tensor_tensor(out=xs, in0=xn[:].rearrange("p j d -> p (j d)"), scalar=0.5,
                                                   in1=xs, op0=ALU.mult, op1=ALU.add).then_inc(s_x, 1)

                def f_bias(t):
                    dve.wait_ge(s_ring_d, 1)
                    dve.sem_inc(s_ring_d, -1)
                    dve.wait_ge(s_x, 1)
                    dve.sem_inc(s_x, -1)
                    xs = x[:, ds(t * TT, TT)]
                    nc.vector.scalar_tensor_tensor(out=xs, in0=b_ring[1][:, :], scalar=1.0 / (WS * WS), in1=xs,
                                                   op0=ALU.mult, op1=ALU.add).then_inc(s_free[1], 1)
                    mark()

                def a_max(r, part, bank):
                    dve.wait_ge(s_ring_d, 1)
                    dve.sem_inc(s_ring_d, -1)
                    if part == 0:
                        o = mx[:, 0, NG * r:NG * r + NG]
                        s = b_ring[bank][:, :].rearrange("p (i k) -> p i k", k=P)
                    else:
                        o = mx[:, 1, NG * r + 2 * part - 2:NG * r + 2 * part]
                        s = b_ring[bank][:, :].rearrange("p (i k) -> p i k", k=SEQ)
                    nc.vector.reduce_max(o, s, AX.X).then_inc(s_free[bank], 1)

                def a_marr():
                    nc.vector.memset(spare[:, 1:2], 0.0).then_inc(s_dve, 1)
                    dve.wait_ge(s_dve, 1)
                    dve.sem_inc(s_dve, -1)
                    for j in range(SB):
                        last = nc.vector.tensor_scalar(marr[:, j, :, :, SLOT],
                                                       mx[:, j, :].rearrange("p (r g) -> p g r", g=NG),
                                                       -1.0, None, ALU.mult)
                    last.then_inc(s_marr, 1)

                def a_m(par, u):
                    dve.wait_ge(s_ring_d, 1)
                    dve.sem_inc(s_ring_d, -1)
                    q = qs[par][:, 2 * u:2 * u + 2, :].rearrange("p g t -> p (g t)")
                    nc.vector.tensor_tensor(q, q, b_ring[u][:, :], ALU.add).then_inc(s_free[u], 1)

                CT = b_pv[:, SEQ:2 * SEQ].rearrange("p (j g c) -> p j g c", j=SB, g=NG)

                def a_inverse():
                    dve.wait_ge(s_ct, 1)
                    dve.sem_inc(s_ct, -1)
                    nc.vector.reciprocal(rden[:], CT[:, :, :, HD]).then_inc(s_div, 1)

                def a_divide(r):
                    dve.wait_ge(s_div, 1)
                    dve.sem_inc(s_div, -1)
                    nc.vector.tensor_tensor(cn[:].rearrange("p j (g r d) -> p j g r d", r=NR, d=HD)[:, :, :, r, :],
                                            CT[:, :, :, 0:HD], rden[:].unsqueeze(3).to_broadcast([P, SB, NG, HD]),
                                            ALU.mult).then_inc(s_cn, 1)

                def a_residual(b):
                    dve.wait_ge(s_ring_d, 1)
                    dve.sem_inc(s_ring_d, -1)
                    dve.wait_ge(s_x, 1)
                    dve.sem_inc(s_x, -1)
                    xs = x[:, ds(b * SEQ, SEQ)]
                    nc.vector.tensor_tensor(xs, b_ring[1][:, 0:SEQ], xs, ALU.add).then_inc(s_free[1], 1)
                    mark()

                def split_w(n):
                    dve.wait_ge(s_wh[n], 1)
                    w, wf = ((w1, w1f), (w2, w2f))[n]
                    nc.vector.scalar_tensor_tensor(out=w[1][:], in0=wf[:], scalar=WS, in1=w[0][:],
                                                   op0=ALU.mult, op1=ALU.subtract).then_inc(s_wl[n], 1)

                def step(st):
                    m, f = st.maxima, st.nxt is not None
                    new = 1 - st.par

                    def weigh_(s):
                        if st.cur is not None:
                            if st.alone and s < E - 1:
                                split_h((s + 1) % 2)
                            weigh(st.cur, st.par, s)

                    if st.tail:
                        a_inverse()
                    if m:
                        a_max(0, 2, 0)
                    if st.tail:
                        a_divide(3)
                    weigh_(0)
                    if m:
                        a_max(0, 0, 0)
                    if st.proj:
                        norm_stats((st.b + 2) * SEQ, SB, a_stats, s_anorm)
                        norm_aggr(SB, a_stats, a_mv, s_anorm)
                        norm_var(a_mv, a_veps, s_anorm, s_avar)
                    if m:
                        a_max(0, 1, 0)
                    if st.tail:
                        a_residual(st.b - 1)
                    if st.proj:
                        norm_apply((st.b + 2) * SEQ, SB, a_mv, a_rstd, a_xn, s_arstd, s_axn)
                    weigh_(1)
                    if m:
                        a_max(1, 0, 0)
                        a_max(1, 1, 1)
                    if f:
                        if st.load:
                            dve.wait_ge(s_xin, st.nxt * 16 + 16)
                            nc.vector.memset(spare[:, 2:3], 0.0).then_inc(s_dve, 1)
                            dve.wait_ge(s_dve, 1)
                            dve.sem_inc(s_dve, -1)
                        norm_stats(st.nxt * TT, TB, stats, s_norm)
                    if st.here:
                        a_inverse()
                    if m:
                        a_max(1, 2, 0)
                    if f:
                        norm_aggr(TB, stats, mv, s_norm)
                    if st.here:
                        a_divide(0)
                    if f:
                        norm_var(mv, veps, s_norm, s_var)
                    if st.opening == 1:
                        split_w(0)
                    weigh_(2)
                    if m:
                        a_max(2, 0, 0)
                        a_max(2, 1, 1)
                    if f:
                        norm_apply(st.nxt * TT, TB, mv, rstd, xn, s_rstd, s_xn)
                    if m:
                        a_max(2, 2, 0)
                    if st.proj:
                        dve.wait_ge(s_qkh, 1)
                        dve.sem_inc(s_qkh, -1)
                        nc.vector.tensor_tensor(qkl[:].rearrange("p a t -> p (a t)"), b_ring[1][:, :],
                                                qkh[:].rearrange("p a t -> p (a t)"),
                                                ALU.subtract).then_inc(s_free[1], 1)
                    weigh_(3)
                    if m:
                        a_max(3, 0, 0)
                    if f:
                        dve.wait_ge(s_xTh, 1)
                        dve.sem_inc(s_xTh, -1)
                        nc.vector.tensor_tensor(xTl[new][:], xT[:], xTh[new][:], ALU.subtract).then_inc(s_free[1], 1)
                    if st.here:
                        a_inverse()
                    if m:
                        a_max(3, 1, 0)
                    if st.here:
                        a_divide(1)
                    if f:
                        gate_max()
                    weigh_(4)
                    if f:
                        gate_shift()
                    if m:
                        a_max(3, 2, 0)
                        a_marr()
                    if f:
                        gate_sum()
                    if st.opening == 1:
                        split_w(1)
                    if f:
                        gate_inverse()
                        gate_probs()
                        largest(2, 3)
                    weigh_(5)
                    if f:
                        equals(2, 3, 3)
                    if m:
                        a_m(new, 0)
                    if f:
                        ranks(3, 4)
                    if st.cur is not None:
                        f_bias(st.cur)
                    if f:
                        largest(4, 4)
                    if st.here:
                        a_inverse()
                    if m:
                        a_m(new, 1)
                    if st.here:
                        a_divide(2)
                    weigh_(6)
                    if f:
                        equals(4, 4, 5)
                        gate_rest()
                        largest(6, 5)
                        equals(6, 5, 7)
                        ranks(7, 8)
                        largest(8, 6)
                        equals(8, 6, 9)
                        gate_total()
                        gate_keep()
                        gate_half()
                        gate_parts(new)
                        gate_low()
                    weigh_(7)
                    if f:
                        f_init(st.nxt)

                for s in s_free + [s_acc, s_cn, s_x]:
                    dve.sem_inc(s, 1)
                run_all(dve, step)

            @block.gpsimd
            def _(pool):
                def rsqrt(s_in, out_, in_, n, s):
                    pool.wait_ge(s_in, 1)
                    pool.sem_inc(s_in, -1)
                    nc.gpsimd.tensor_tensor(out_[:], in_[:], neg_half[:, 0:n], ALU.pow).then_inc(s, 1)

                def split_h(par, halves):
                    for c in halves:
                        pool.wait_ge(s_hf[c], 1)
                        pool.sem_inc(s_hf[c], -1)
                        nc.gpsimd.tensor_tensor(hl[par][:, c, :], hf[par][:, c, :], hh[par][:, c, :],
                                                ALU.subtract).then_inc(s_h[c], 1)

                def causal(r, part):
                    pool.wait_ge(s_e, 1)
                    pool.sem_inc(s_e, -1)
                    n, w = (4, P) if part == 2 else (2, SEQ)
                    v = pt[r % 2][:, part, :].rearrange("p (i q) -> p i q", q=w)[:, :, 0:P]
                    nc.gpsimd.affine_select(out=v, in_=v, compare_op=ALU.is_ge, fill=0.0, base=0,
                                            pattern=[[0, n], [1, P]], channel_multiplier=-1).then_inc(s_p, 1)

                def step(st):
                    for s in range(E):
                        if s % 2 == 0 and st.here:
                            causal(s // 2, 0)
                        if st.cur is not None and s < E - 1:
                            split_h((s + 1) % 2, (0,) if st.alone else (0, 1))
                        if st.nxt is not None and s == E - 1:
                            split_h(0, (0, 1))
                        if s == 2 and st.nxt is not None:
                            rsqrt(s_var, rstd, veps, TB, s_rstd)
                        if s % 2 == 0 and st.here:
                            causal(s // 2, 1)
                            causal(s // 2, 2)
                        if s == 0 and st.proj:
                            rsqrt(s_avar, a_rstd, a_veps, SB, s_arstd)

                for c in range(HC):
                    pool.sem_inc(s_h[c], 1)
                pool.sem_inc(s_p, 2)
                run_all(pool, step)


_INS = ['L0_attn_x', 'L0_attn_q_proj', 'L0_attn_k_proj', 'L0_attn_v_proj', 'L0_attn_out_proj', 'L0_ffn_gate_W',
        'L0_ffn_W1', 'L0_ffn_b1', 'L0_ffn_W2', 'L0_ffn_b2']
_OUTS = [((32, 256, 128), 'float32')]


def kernel(**inputs):
    import numpy as _np
    import concourse.bacc as _bacc
    from concourse import mybir as _mybir
    from concourse.bass_utils import run_bass_kernel_spmd as _run

    nc = _bacc.Bacc("TRN2", target_bir_lowering=False, num_devices=1)
    arrays, args = {}, []
    for name in _INS:
        a = _np.ascontiguousarray(inputs[name])
        arrays[f"in_{name}_dram"] = a
        args.append(nc.dram_tensor(f"in_{name}_dram", a.shape, _mybir.dt.from_np(a.dtype), kind="ExternalInput").ap())
    for i, (shape, dtype) in enumerate(_OUTS):
        dt = _mybir.dt.from_np(_np.dtype(dtype))
        args.append(nc.dram_tensor(f"out_{i}_dram", shape, dt, kind="ExternalOutput").ap())
    build(nc, *args)
    r = _run(nc, [arrays], core_ids=[0])
    return r.results[0]["out_0_dram"]
```

```python
import concourse.bass as bass
from concourse import mybir
from contextlib import ExitStack


fp32 = mybir.dt.float32
fp16 = mybir.dt.float16
bf16 = mybir.dt.bfloat16
ALU = mybir.AluOpType
ACT = mybir.ActivationFunctionType
AX = mybir.AxisListType

P = 128
NB, SEQ, D = 32, 256, 128
SB = SEQ // P
NBLK = NB * SB
E, HID = 8, 256
HC = HID // P
TB = 4
TT = TB * P
NT = NBLK // TB
H, HD = 16, 8
NG, NR = 4, 4
SLOT = 3 * HD
EPS = 1e-5
SCALE = 1.0 / float(HD) ** 0.5
WS = 8.0
BIG = -1.0e30


def ds(start, size):
    return bass.ds(start, size)


class Step:

    def __init__(self, b, par, buf, cur, nxt, load, tail=True, here=True, maxima=True, proj=True, settle=False,
                 second=False, first_of_loop=False, opening=0):
        self.b, self.par, self.buf, self.cur, self.nxt, self.load = b, par, buf, cur, nxt, load
        self.tail, self.here, self.maxima, self.proj, self.settle = tail, here, maxima, proj, settle
        self.alone = not (here or maxima)
        self.second, self.first_of_loop, self.opening = second, first_of_loop, opening
        self.run = [None if cur is None else e for e in range(E)]
        self.fore = [None if cur is None else (buf, e) for e in range(1, E)] + [None if nxt is None else (1 - buf, 0)]


NONE = dict(tail=False, here=False, maxima=False, proj=False)


def fixed_step(b):
    even = b % 2 == 0
    cur, buf = {-2: (None, 1), -1: (1, 0), 0: (2, 1), 1: (None, 1)}.get(b, (b // 2 + 2 if even else b // 2 - 1, b % 2))
    nxt = b // 2 - 1 if even else b // 2 + 3
    return Step(b, b % 2, buf, cur if cur is not None and cur < NT else None, nxt if 0 <= nxt < NT else None,
                not even, tail=1 <= b <= NB, here=0 <= b < NB, maxima=-1 <= b < NB - 1, proj=-2 <= b < NB - 2,
                settle=b >= NB - 1, second=not even and b > 1)


def loop_steps(i):
    return [Step(i * 2, 0, 0, i + 2, i - 1, False, first_of_loop=True),
            Step(i * 2 + 1, 1, 1, i - 1, i + 3, True, second=True)]


def run_all(eng, step):
    step(Step(-4, 0, 0, None, 0, True, opening=1, **NONE))
    step(Step(-3, 1, 1, 0, 1, True, opening=2, **NONE))
    for b in range(-2, 2):
        step(fixed_step(b))
    with eng.Fori(1, NT - 3) as i:
        for st in loop_steps(i):
            step(st)
    for b in range(NB - 6, NB + 2):
        step(fixed_step(b))


def build(nc, x_in, q_proj, k_proj, v_proj, out_proj, gate_w, w1_in, b1_in, w2_in, b2_in, out):
    xin_v = x_in.rearrange("b (k p) d -> p (b k) d", p=P)
    out_v = out.rearrange("b (k p) d -> p (b k) d", p=P)
    ctx = ExitStack()
    with ctx:
        def sb(name, shape, dt):
            return ctx.enter_context(nc.sbuf_tensor(name, shape, dt))

        def sem(name):
            return ctx.enter_context(nc.semaphore(name))

        x = sb("x", [P, NBLK * D], fp32)
        ident = sb("ident", [P, P], fp32)
        ident_h = sb("ident_h", [P, P], fp16)
        ident_b = sb("ident_b", [P, P], bf16)
        gwf = sb("gwf", [P, E], fp32)
        gw = [sb(f"gw_{k}", [P, E], fp16) for k in ("hi", "lo")]
        w1f = sb("w1f", [P, E * HID], fp32)
        w1 = [sb(f"w1_{k}", [P, E * HID], fp16) for k in ("hi", "lo")]
        w2f = sb("w2f", [P, E * HC * D], fp32)
        w2 = [sb(f"w2_{k}", [P, E * HC * D], fp16) for k in ("hi", "lo")]
        b1r = sb("b1r", [E * HC, P], fp32)
        b1 = sb("b1", [P, E * HC], fp32)
        b2f = sb("b2f", [96, D], fp32)
        b2 = sb("b2", [96, D], fp16)
        waf = sb("waf", [P, 3 * D], fp32)
        wa = [sb(f"wa_{k}", [P, 3 * D], fp16) for k in ("hi", "lo")]
        wo = sb("wo", [P, D], fp32)
        mask = sb("mask", [P, NG, P], bf16)
        neg_half = sb("neg_half", [P, TB], fp32)
        order = sb("order", [P, TB, E], fp32)
        sel = {k: sb(f"sel_{k}", [P, NG, NR, 4, HD], fp16) for k in ("qh", "ql", "kh", "kl")}
        SLOTS = {"qh": (0, 1), "ql": (2,), "kh": (0, 2), "kl": (1,)}
        kones = sb("kones", [P, 1], fp32)

        stats = sb("stats", [P, TB, 6], fp32)
        mv = sb("mv", [P, TB, 2], fp32)
        veps = sb("veps", [P, TB], fp32)
        rstd = sb("rstd", [P, TB], fp32)
        xn = sb("xn", [P, TB, D], fp32)
        xTh = [sb(f"xTh{i}", [P, TT], fp16) for i in range(2)]
        xTl = [sb(f"xTl{i}", [P, TT], fp16) for i in range(2)]
        small = sb("small", [P, 9, TB], fp32)
        wide = sb("wide", [P, 10, TB, E], fp32)
        cw = [sb(f"cw{i}", [P, TB, E], fp32) for i in range(2)]
        half = sb("half", [P, TB, E], fp32)
        cw3 = sb("cw3", [P, TB, 3, 32], fp16)
        cwT = sb("cwT", [96, TT], fp16)
        hf = [sb(f"hf{i}", [P, HC, TT], fp32) for i in range(2)]
        hh = [sb(f"hh{i}", [P, HC, TT], fp16) for i in range(2)]
        hl = [sb(f"hl{i}", [P, HC, TT], fp16) for i in range(2)]
        spare = sb("spare", [P, 4 + NR], fp32)
        masked = sb("masked", [P, NR, NG, P], fp32)

        a_stats = sb("a_stats", [P, SB, 6], fp32)
        a_mv = sb("a_mv", [P, SB, 2], fp32)
        a_veps = sb("a_veps", [P, SB], fp32)
        a_rstd = sb("a_rstd", [P, SB], fp32)
        a_xn = sb("a_xn", [P, SB, D], fp32)
        a_xTh = sb("a_xTh", [P, SEQ], fp16)
        a_xTl = sb("a_xTl", [P, SEQ], fp16)
        qkh = sb("qkh", [P, 2, SEQ], fp16)
        qkl = sb("qkl", [P, 2, SEQ], fp16)
        qs = [sb(f"qs{i}", [P, NG, SEQ], fp16) for i in range(2)]
        ks = [sb(f"ks{i}", [P, NG, SEQ], fp16) for i in range(2)]
        va = [sb(f"va{i}", [P, SB, H, 32], fp32) for i in range(2)]

        def va_chunks(v):
            return v[:].rearrange("p j (n h) (u d) -> p j n (h u) d", h=2, d=HD)

        mx = sb("mx", [P, SB, NR * NG], fp32)
        marr = sb("marr", [P, SB, NG, NR, 4 * HD], fp16)
        pt = [sb(f"pt{i}", [P, 3, 512], fp32) for i in range(2)]
        cT = sb("cT", [P, SEQ], fp32)
        rden = sb("rden", [P, SB * NG, 2], fp32)
        cn = sb("cn", [P, SB * D], fp32)
        cnT = sb("cnT", [P, SEQ], fp32)

        ps = [ctx.enter_context(nc.psum_tensor(f"bank{i}", [P, 512], fp32)) for i in range(8)]
        b_z, b_y, b_ring, b_s, b_pv = ps[0:2], ps[2], ps[3:5], ps[5:7], ps[7]

        s_xin = sem("x_loaded")
        s_store = sem("x_final")
        s_out = sem("x_stored")
        s_var = sem("var")
        s_rstd = sem("rstd")
        s_xn = sem("xn")
        s_xTh = sem("xTh")
        s_shift = sem("shift")
        s_exp = sem("exp")
        s_cw = sem("cw")
        s_z = sem("z")
        s_hf = [sem(f"hf{c}") for c in range(HC)]
        s_hfd = sem("hfd")
        s_h = [sem(f"h{c}") for c in range(HC)]
        s_y = sem("y")
        s_acc = sem("acc")
        s_avar = sem("a_var")
        s_arstd = sem("a_rstd")
        s_axn = sem("a_xn")
        s_ring_a = sem("ring_a")
        s_ring_d = sem("ring_d")
        s_free = [sem(f"free{i}") for i in range(2)]
        s_axTh = sem("a_xTh")
        s_qkh = sem("qkh")
        s_marr = sem("marr")
        s_s = sem("s")
        s_e = sem("e")
        s_p = sem("p")
        s_pv = sem("pv")
        s_cT = sem("cT")
        s_ct = sem("ct")
        s_cn = sem("cn")
        s_dve = sem("dve")
        s_x = sem("x")
        s_norm = sem("norm")
        s_anorm = sem("a_norm")
        s_gate = sem("gate")
        s_masked = sem("masked")
        s_div = sem("div")

        w_in = [sem(f"w_in{i}") for i in range(4)]
        s_zero, s_ident, s_b1 = sem("zero"), sem("ident"), sem("b1_t")
        s_wh = [sem(f"w{n + 1}_high") for n in range(2)]
        s_wa = sem("wa_low")
        s_wl = [sem(f"w{n + 1}_low") for n in range(2)]
        s_izero, s_vzero, s_own = sem("ident_zero"), sem("va_zero"), sem("own")

        with nc.Block() as block:
            @block.sync
            def _(sp):
                sp.dma_start(x[:, 0:TT].rearrange("p (k d) -> p k d", d=D), xin_v[:, 0:TB, :]).then_inc(s_xin, 16)
                for dst, src in ((b1r, b1_in.rearrange("e (c p) -> (e c) p", p=P)), (gwf, gate_w)):
                    sp.dma_start(dst[:], src).then_inc(w_in[2], 16)
                sp.wait_ge(s_zero, 1)
                for k in range(3):
                    sp.dma_start(b2f[32 * k:32 * k + E, :], b2_in).then_inc(w_in[2], 16)
                sp.dma_start(w1f[:].rearrange("d (e h) -> d e h", e=E),
                             w1_in.rearrange("e d h -> d e h")).then_inc(w_in[0], 16)
                sp.dma_start(w2f[:].rearrange("p (n o) -> p n o", o=D),
                             w2_in.rearrange("e (c p) o -> p (e c) o", p=P)).then_inc(w_in[1], 16)
                for dst, src in ((waf[:, 0:D], q_proj), (waf[:, D:2 * D], k_proj), (waf[:, 2 * D:3 * D], v_proj),
                                 (wo[:], out_proj)):
                    sp.dma_start(dst, src).then_inc(w_in[3], 16)
                sp.wait_ge(s_xin, 16)
                sp.wait_ge(w_in[2], 80)

            @block.gpsimd
            def _(pool):
                nc.gpsimd.memset(ident[:], 0.0)
                nc.gpsimd.memset(mask[:], 0.0).then_inc(s_izero, 1)
                nc.gpsimd.memset(neg_half[:], -0.5)
                for e in range(E):
                    nc.gpsimd.memset(order[:, :, e], float(E - e))
                pool.wait_ge(s_izero, 1)
                nc.gpsimd.affine_select(out=ident[:], in_=ident[:], compare_op=ALU.not_equal, fill=1.0, base=0,
                                        pattern=[[-1, P]], channel_multiplier=1).then_inc(s_ident, 1)
                nc.gpsimd.affine_select(out=mask[:], in_=mask[:], compare_op=ALU.is_ge, fill=BIG, base=0,
                                        pattern=[[0, NG], [-1, P]], channel_multiplier=1)
                nc.gpsimd.memset(marr[:], 0.0)
                nc.gpsimd.memset(va[0][:], 0.0)
                nc.gpsimd.memset(va[1][:], 0.0).then_inc(s_vzero, 1)
                pool.wait_ge(s_vzero, 1)
                for i in range(2):
                    nc.gpsimd.memset(va_chunks(va[i])[:, :, :, 1:8:6, 0:1], 1.0)

            @block.tensor
            def _(pe):
                pe.wait_ge(s_ident, 1)
                pe.wait_ge(w_in[2], 80)
                nc.tensor.transpose(ps[0][:, 0:E * HC], b1r[:], ident[0:E * HC, 0:E * HC]).then_inc(s_b1, 1)

            @block.vector
            def _(dve):
                nc.vector.memset(b2f[:], 0.0).then_inc(s_zero, 1)
                nc.vector.memset(cw3[:], 0.0)
                for k in sel:
                    last = nc.vector.memset(sel[k][:], 0.0)
                last.then_inc(s_own, 1)
                dve.wait_ge(s_own, 1)
                dve.sem_inc(s_own, -1)
                dve.wait_ge(s_ident, 1)
                nc.vector.reduce_sum(kones[:], ident[:].rearrange("p (i r) -> p i r", r=32)[:, :, SLOT], AX.X)
                nc.vector.tensor_copy(ident_b[:], ident[:])
                nc.vector.tensor_copy(ident_h[:], ident[:]).then_inc(s_dve, 1)
                dve.wait_ge(s_dve, 1)
                dve.sem_inc(s_dve, -1)
                for k, slots in SLOTS.items():
                    for g in range(NG):
                        for s in slots:
                            nc.vector.tensor_copy(sel[k][:, g, :, s, :],
                                                  ident_h[:, 32 * g:32 * g + 32].rearrange("p (i d) -> p i d", d=HD))
                dve.wait_ge(s_b1, 1)
                nc.vector.tensor_scalar(b1[:], ps[0][:, 0:E * HC], WS, None, ALU.mult)
                nc.vector.tensor_scalar(b2[:], b2f[:], WS * WS, None, ALU.mult).then_inc(s_own, 1)
                nc.vector.tensor_scalar(gw[0][:], gwf[:], WS, None, ALU.mult).then_inc(s_own, 1)
                dve.wait_ge(s_own, 2)
                nc.vector.scalar_tensor_tensor(out=gw[1][:], in0=gwf[:], scalar=WS, in1=gw[0][:],
                                               op0=ALU.mult, op1=ALU.subtract)
                nc.vector.scalar_tensor_tensor(out=b2[64:96, :], in0=b2f[64:96, :], scalar=WS * WS,
                                               in1=b2[64:96, :], op0=ALU.mult, op1=ALU.subtract)

        with nc.Block() as block:
            @block.sync
            def _(sp):
                with sp.Fori(1, NT) as t:
                    sp.wait_ge(s_xin, t * 16)
                    sp.dma_start(x[:, ds(t * TT, TT)].rearrange("p (k d) -> p k d", d=D),
                                 xin_v[:, ds(t * TB, TB), :]).then_inc(s_xin, 16)
                sp.wait_ge(s_store, 1)
                sp.sem_inc(s_store, -1)
                with sp.Fori(0, NT) as t:
                    sp.wait_ge(s_store, 1)
                    sp.sem_inc(s_store, -1)
                    sp.dma_start(out_v[:, ds(t * TB, TB), :],
                                 x[:, ds(t * TT, TT)].rearrange("p (k d) -> p k d", d=D)).then_inc(s_out, 16)
                sp.wait_ge(s_out, NT * 16)

            @block.tensor
            def _(pe):
                def first_product(par, e):
                    for c in range(HC):
                        pe.wait_ge(s_h[c], 1)
                        pe.sem_inc(s_h[c], -1)
                        w = slice(e * HID + c * P, e * HID + (c + 1) * P)
                        nc.tensor.matmul(b_z[c][:, :], w1[0][:, w], xTh[par][:], start=True, stop=False)
                        nc.tensor.matmul(b_z[c][:, :], w1[0][:, w], xTl[par][:], start=False, stop=False)
                        nc.tensor.matmul(b_z[c][:, :], w1[1][:, w], xTh[par][:],
                                         start=False, stop=True).then_inc(s_z, 1)

                def second_product(e, followed, final):
                    if not followed:
                        for c in range(HC):
                            pe.wait_ge(s_h[c], 1)
                    pe.wait_ge(s_acc, 1)
                    pe.sem_inc(s_acc, -1)
                    if final:
                        pe.sem_inc(s_store, 1)
                    for j in range(TB):
                        o, t = b_y[:, j * P:(j + 1) * P], slice(j * P, (j + 1) * P)
                        for c in range(HC):
                            w = slice((e * HC + c) * D, (e * HC + c + 1) * D)
                            nc.tensor.matmul(o, hh[e % 2][:, c, t], w2[0][:, w], start=(c == 0), stop=False)
                            nc.tensor.matmul(o, hh[e % 2][:, c, t], w2[1][:, w], start=False, stop=False)
                            last = nc.tensor.matmul(o, hl[e % 2][:, c, t], w2[0][:, w],
                                                    start=False, stop=(c == HC - 1))
                    last.then_inc(s_y, 1)

                def blocks(bank, n=SB):
                    return [b_ring[bank][:, j * P:(j + 1) * P] for j in range(n)]

                def f_tr():
                    pe.wait_ge(s_xn, 1)
                    pe.sem_inc(s_xn, -1)
                    pe.wait_ge(s_free[1], 1)
                    pe.sem_inc(s_free[1], -1)
                    for j, o in enumerate(blocks(1, TB)):
                        last = nc.tensor.transpose(o, xn[:, j, :], ident[:])
                    last.then_inc(s_ring_a, 1)

                def f_logit(par):
                    pe.wait_ge(s_free[1], 1)
                    pe.sem_inc(s_free[1], -1)
                    for j in range(TB):
                        o, t = b_ring[1][:, j * E:(j + 1) * E], slice(j * P, (j + 1) * P)
                        nc.tensor.matmul(o, xTh[par][:, t], gw[0][:], start=True, stop=False)
                        nc.tensor.matmul(o, xTh[par][:, t], gw[1][:], start=False, stop=False)
                        last = nc.tensor.matmul(o, xTl[par][:, t], gw[0][:], start=False, stop=True)
                    last.then_inc(s_ring_d, 1)

                def f_cwT():
                    pe.wait_ge(s_cw, 1)
                    pe.sem_inc(s_cw, -1)
                    pe.wait_ge(s_free[1], 1)
                    pe.sem_inc(s_free[1], -1)
                    for j in range(TB):
                        last = nc.tensor.matmul(b_ring[1][0:96, j * P:(j + 1) * P],
                                                cw3[:, j].rearrange("p k e -> p (k e)"), ident_h[:],
                                                start=True, stop=True)
                    last.then_inc(s_ring_a, 1)

                def f_bias():
                    pe.wait_ge(s_free[1], 1)
                    pe.sem_inc(s_free[1], -1)
                    for j, o in enumerate(blocks(1, TB)):
                        last = nc.tensor.matmul(o, cwT[:, j * P:(j + 1) * P], b2[:], start=True, stop=True)
                    last.then_inc(s_ring_d, 1)

                def a_tr():
                    pe.wait_ge(s_axn, 1)
                    pe.sem_inc(s_axn, -1)
                    pe.wait_ge(s_free[1], 1)
                    pe.sem_inc(s_free[1], -1)
                    for j, o in enumerate(blocks(1)):
                        last = nc.tensor.transpose(o, a_xn[:, j, :], ident[:])
                    last.then_inc(s_ring_a, 1)

                def a_qk():
                    pe.wait_ge(s_free[1], 1)
                    pe.sem_inc(s_free[1], -1)
                    for i in range(2):
                        o, w = b_ring[1][:, i * SEQ:(i + 1) * SEQ], slice(i * D, (i + 1) * D)
                        nc.tensor.matmul(o, wa[0][:, w], a_xTh[:], start=True, stop=False)
                        nc.tensor.matmul(o, wa[0][:, w], a_xTl[:], start=False, stop=False)
                        last = nc.tensor.matmul(o, wa[1][:, w], a_xTh[:], start=False, stop=True)
                    last.then_inc(s_ring_a, 1)

                def a_stack(u):
                    bank, i, half = 1 - u % 2, u % 2, u // 2
                    pe.wait_ge(s_free[bank], 1)
                    pe.sem_inc(s_free[bank], -1)
                    for g in range(2):
                        o = b_ring[bank][:, g * SEQ:(g + 1) * SEQ]
                        hi, lo = (sel[k][:, 2 * half + g].rearrange("p i s d -> p (i s d)")
                                  for k in (("qh", "ql"), ("kh", "kl"))[i])
                        nc.tensor.matmul(o, hi, qkh[:, i, :], start=True, stop=False)
                        last = nc.tensor.matmul(o, lo, qkl[:, i, :], start=False, stop=True)
                    last.then_inc(s_ring_a, 1)

                def a_v():
                    pe.wait_ge(s_free[1], 1)
                    pe.sem_inc(s_free[1], -1)
                    for j, o in enumerate(blocks(1)):
                        t, w = slice(j * P, (j + 1) * P), slice(2 * D, 3 * D)
                        nc.tensor.matmul(o, a_xTh[:, t], wa[0][:, w], start=True, stop=False)
                        nc.tensor.matmul(o, a_xTh[:, t], wa[1][:, w], start=False, stop=False)
                        last = nc.tensor.matmul(o, a_xTl[:, t], wa[0][:, w], start=False, stop=True)
                    last.then_inc(s_ring_a, 1)

                def a_max(par, r, part, bank):
                    pe.wait_ge(s_free[bank], 1)
                    pe.sem_inc(s_free[bank], -1)
                    rows = slice(32 * r, 32 * r + 32)
                    o = b_ring[bank]
                    for n, g in enumerate(range(NG) if part == 0 else (2 * part - 2, 2 * part - 1)):
                        if part == 0:
                            last = nc.tensor.matmul(o[:, n * P:(n + 1) * P], qs[par][rows, g, 0:P],
                                                    ks[par][rows, g, 0:P], start=True, stop=True,
                                                    tile_position=(32 * r, 0))
                        else:
                            nc.tensor.matmul(o[:, n * SEQ:(n + 1) * SEQ], qs[par][rows, g, P:SEQ],
                                             ks[par][rows, g, :], start=True, stop=False,
                                             tile_position=(32 * r, 0), skip_group_check=True)
                    if part > 0:
                        o, m = o[:, :].rearrange("p (i k) -> p i k", k=SEQ)[:, :, P:SEQ], mask[:, 0:2, :]
                        last = nc.tensor.matmul(o, ident_b[:], m, start=False, stop=True, skip_group_check=True)
                    last.then_inc(s_ring_d, 1)

                def a_m(u):
                    if u == 0:
                        pe.wait_ge(s_marr, 1)
                        pe.sem_inc(s_marr, -1)
                    pe.wait_ge(s_free[u], 1)
                    pe.sem_inc(s_free[u], -1)
                    for g in range(2):
                        for j in range(SB):
                            o = b_ring[u][:, g * SEQ + j * P:g * SEQ + (j + 1) * P]
                            last = nc.tensor.matmul(o, marr[:, j, 2 * u + g].rearrange("p i r -> p (i r)"),
                                                    ident_h[:], start=True, stop=True)
                    last.then_inc(s_ring_d, 1)

                def a_scores(par, r, part):
                    pe.wait_ge(s_p, 1)
                    pe.sem_inc(s_p, -1)
                    rows = slice(32 * r, 32 * r + 32)
                    bank = b_s[(3 * r + part) % 2]
                    for n, g in enumerate(range(NG) if part == 2 else (2 * part, 2 * part + 1)):
                        if part == 2:
                            last = nc.tensor.matmul(bank[:, n * P:(n + 1) * P], ks[par][rows, g, P:SEQ],
                                                    qs[par][rows, g, P:SEQ], start=True, stop=True,
                                                    tile_position=(32 * r, 0))
                        else:
                            last = nc.tensor.matmul(bank[:, n * SEQ:(n + 1) * SEQ], ks[par][rows, g, 0:P],
                                                    qs[par][rows, g, :], start=True, stop=True,
                                                    tile_position=(32 * r, 0))
                    last.then_inc(s_s, 1)

                def a_pv(par, r):
                    pe.wait_ge(s_p, 2)
                    if r % 2 == 0:
                        pe.wait_ge(s_cn, 1)
                        pe.sem_inc(s_cn, -1)
                    for g in range(NG):
                        nc.tensor.matmul(b_pv[32 * g:32 * g + 32, 0:SEQ], va[par][:, 0, NR * g + r, :],
                                         pt[r % 2][:, g // 2, (g % 2) * SEQ:(g % 2 + 1) * SEQ],
                                         start=(r % 2 == 0), stop=False, tile_position=(0, 32 * g),
                                         skip_group_check=True)
                    for g in range(NG):
                        last = nc.tensor.matmul(b_pv[32 * g:32 * g + 32, P:SEQ], va[par][:, 1, NR * g + r, :],
                                                pt[r % 2][:, 2, g * P:(g + 1) * P], start=False,
                                                stop=(r % 2 == 1), tile_position=(0, 32 * g),
                                                skip_group_check=True)
                    if r % 2 == 1:
                        last.then_inc(s_pv, 1)

                def a_ct():
                    pe.wait_ge(s_cT, 1)
                    pe.sem_inc(s_cT, -1)
                    for j in range(SB):
                        last = nc.tensor.transpose(b_pv[:, SEQ + j * P:SEQ + (j + 1) * P],
                                                   cT[:, j * P:(j + 1) * P], ident[:])
                    last.then_inc(s_ct, 1)

                def a_tail_a():
                    pe.wait_ge(s_cn, 1)
                    pe.wait_ge(s_free[1], 1)
                    pe.sem_inc(s_free[1], -1)
                    for j, o in enumerate(blocks(1)):
                        last = nc.tensor.transpose(o, cn[:, j * D:(j + 1) * D], ident[:])
                    last.then_inc(s_ring_a, 1)

                def a_tail_b():
                    pe.wait_ge(s_free[1], 1)
                    pe.sem_inc(s_free[1], -1)
                    for j, o in enumerate(blocks(1)):
                        last = nc.tensor.matmul(o, cnT[:, j * P:(j + 1) * P], wo[:], start=True, stop=True)
                    last.then_inc(s_ring_d, 1)

                def ahead(st, s):
                    if s == 0 and st.here and st.settle:
                        for k in range(2):
                            pe.wait_ge(s_free[k], 1)
                    if s % 2 == 0 and st.here:
                        a_scores(st.par, s // 2, 0)
                        a_scores(st.par, s // 2, 1)
                    if s == 6 and st.cur is not None:
                        f_bias()

                def between(st, s):
                    m, other = st.maxima, 1 - st.par
                    if s in (0, 4) and (st.here if s else st.tail):
                        a_ct()
                    if s == 0:
                        if m:
                            a_max(other, 0, 2, 0)
                    if s == 1:
                        if m:
                            a_max(other, 0, 1, 0)
                        if st.tail:
                            a_tail_b()
                    if s == 2:
                        if m:
                            a_max(other, 1, 2, 0)
                        if st.proj:
                            a_tr()
                    if s == 3:
                        if m:
                            a_max(other, 2, 2, 0)
                        if st.proj:
                            a_qk()
                    if s == 4:
                        if m:
                            a_max(other, 3, 1, 0)
                        if st.nxt is not None:
                            f_logit(1 - st.buf)
                    if s == 5 and st.cur is not None:
                        f_cwT()
                    if s == 6 and m:
                        a_m(0)
                        a_m(1)
                    if s == 7 and st.proj:
                        a_stack(2)
                        a_stack(3)

                def behind(st, s):
                    par, m, other = st.par, st.maxima, 1 - st.par
                    if s % 2 == 0 and st.here:
                        a_scores(par, s // 2, 2)
                    if s % 2 == 1 and st.here:
                        a_pv(par, s // 2)
                    if s == 3 and st.nxt is not None:
                        f_tr()
                    if s == 0:
                        if m:
                            a_max(other, 0, 0, 0)
                        if st.tail:
                            a_tail_a()
                    if s in (1, 2) and m:
                        a_max(other, s, 0, 0)
                        a_max(other, s, 1, 1)
                    if s == 3 and m:
                        a_max(other, 3, 0, 0)
                    if s == 4 and m:
                        a_max(other, 3, 2, 0)
                    if s == 6 and st.proj:
                        a_stack(0)
                        a_stack(1)
                    if s == 7 and st.proj:
                        a_v()

                state = {"second": False}

                def step(st):
                    for s in range(E):
                        ahead(st, s)
                        if s == E - 1 and st.opening == 1:
                            pe.wait_ge(s_wl[0], 1)
                        if s == 0 and st.opening == 2:
                            pe.wait_ge(s_wl[1], 1)
                        if s == E - 1 and st.opening == 2:
                            pe.wait_ge(s_wa, 1)
                        if st.fore[s] is not None:
                            first_product(*st.fore[s])
                        between(st, s)
                        e = st.run[s]
                        if e is not None:
                            second_product(e, st.fore[s] is not None,
                                           e == 0 and (state["second"] or st.first_of_loop))
                            state["second"] = e == E - 1 and st.second
                        behind(st, s)

                run_all(pe, step)
                pe.wait_ge(s_acc, 1)
                pe.sem_inc(s_acc, -1)
                pe.sem_inc(s_store, 1)

            @block.scalar
            def _(act):
                def relu(c, e, done):
                    act.wait_ge(s_z, 1)
                    act.sem_inc(s_z, -1)
                    b = b1[:, e * HC + c:e * HC + c + 1]
                    nc.scalar.activation(hh[e % 2][:, c, :], b_z[c][:, :], ACT.Relu, bias=b)
                    nc.scalar.activation(hf[e % 2][:, c, :], b_z[c][:, :], ACT.Relu, bias=b).then_inc(done, 1)

                def exp(r, part):
                    act.wait_ge(s_s, 1)
                    act.sem_inc(s_s, -1)
                    nc.scalar.activation(pt[r % 2][:, part, :], b_s[(3 * r + part) % 2][:, :], ACT.Exp,
                                         scale=SCALE).then_inc(s_e, 1)

                def contexts():
                    act.wait_ge(s_pv, 1)
                    act.sem_inc(s_pv, -1)
                    nc.scalar.copy(cT[:], b_pv[:, 0:SEQ]).then_inc(s_cT, 1)

                def stack(par, u):
                    act.wait_ge(s_ring_a, 1)
                    act.sem_inc(s_ring_a, -1)
                    bank, half = 1 - u % 2, u // 2
                    if u % 2 == 0:
                        nc.scalar.copy(qs[par][:, 2 * half:2 * half + 2, :].rearrange("p g t -> p (g t)"),
                                       b_ring[bank][:, :]).then_inc(s_free[bank], 1)
                    else:
                        nc.scalar.activation(ks[par][:, 2 * half:2 * half + 2, :].rearrange("p g t -> p (g t)"),
                                             b_ring[bank][:, :], ACT.Identity,
                                             bias=kones[:, 0:1]).then_inc(s_free[bank], 1)

                def step(st):
                    for s in range(E):
                        if s in (0, 4) and (st.here if s else st.tail):
                            contexts()
                        if s % 2 == 0 and st.here:
                            exp(s // 2, 0)
                        if st.fore[s] is not None:
                            relu(0, st.fore[s][1], s_hf[0])
                        if s == 2 and st.proj:
                            act.wait_ge(s_ring_a, 1)
                            act.sem_inc(s_ring_a, -1)
                            nc.scalar.copy(a_xTh[:], b_ring[1][:, 0:SEQ]).then_inc(s_axTh, 1)
                        if st.fore[s] is not None:
                            e = st.fore[s][1]
                            relu(1, e, s_hfd if st.alone and e > 1 else s_hf[1])
                        if s % 2 == 0 and st.here:
                            exp(s // 2, 1)
                        if s == 3 and st.proj:
                            act.wait_ge(s_ring_a, 1)
                            act.sem_inc(s_ring_a, -1)
                            nc.scalar.activation(qkh[:].rearrange("p a t -> p (a t)"), b_ring[1][:, :], ACT.Copy,
                                                 scale=1.0 / WS).then_inc(s_qkh, 1)
                        if s == 5 and st.cur is not None:
                            act.wait_ge(s_ring_a, 1)
                            act.sem_inc(s_ring_a, -1)
                            nc.scalar.copy(cwT[:], b_ring[1][0:96, :]).then_inc(s_free[1], 1)
                        if s == 7 and st.proj:
                            stack(st.par, 2)
                            stack(st.par, 3)
                        if s % 2 == 0 and st.here:
                            exp(s // 2, 2)
                        if s == 0 and st.tail:
                            act.wait_ge(s_ring_a, 1)
                            act.sem_inc(s_ring_a, -1)
                            nc.scalar.copy(cnT[:], b_ring[1][:, 0:SEQ]).then_inc(s_free[1], 1)
                        if s == 3 and st.nxt is not None:
                            act.wait_ge(s_ring_a, 1)
                            act.sem_inc(s_ring_a, -1)
                            nc.scalar.copy(xTh[1 - st.buf][:], b_ring[1][:, :]).then_inc(s_xTh, 1)
                        if s == 3 and st.opening == 1:
                            act.wait_ge(w_in[1], 16)
                            nc.scalar.activation(w2[0][:], w2f[:], ACT.Copy, scale=WS).then_inc(s_wh[1], 1)
                        if s == 4 and st.nxt is not None:
                            act.wait_ge(s_shift, 1)
                            act.sem_inc(s_shift, -1)
                            nc.scalar.activation(wide[:, 1], wide[:, 0], ACT.Exp,
                                                 scale=1.0 / WS).then_inc(s_exp, 1)
                        if s == 6 and st.proj:
                            stack(st.par, 0)
                            stack(st.par, 1)
                        if s == 7 and st.proj:
                            act.wait_ge(s_ring_a, 1)
                            act.sem_inc(s_ring_a, -1)
                            for j in range(SB):
                                last = nc.scalar.activation(
                                    va_chunks(va[st.par])[:, j, :, 0:7:6, :],
                                    b_ring[1][:, j * P:(j + 1) * P].rearrange("p (n h d) -> p n h d", h=2, d=HD),
                                    ACT.Copy, scale=1.0 / WS)
                            last.then_inc(s_free[1], 1)

                act.wait_ge(w_in[0], 16)
                nc.scalar.activation(w1[0][:], w1f[:], ACT.Copy, scale=WS).then_inc(s_wh[0], 1)
                run_all(act, step)

            @block.vector
            def _(dve):
                def mark():
                    nc.vector.memset(spare[:, 0:1], 0.0).then_inc(s_x, 1)

                def norm_stats(base, n, st_, s):
                    dve.wait_ge(s_x, 1)
                    for j in range(n):
                        last = nc.vector.bn_stats(st_[:, j, :], x[:, ds(base + j * P, P)])
                    last.then_inc(s, 1)

                def norm_aggr(n, st_, mv_, s):
                    dve.wait_ge(s, 1)
                    dve.sem_inc(s, -1)
                    for j in range(n):
                        last = nc.vector.bn_aggr(mv_[:, j, :], st_[:, j, :])
                    last.then_inc(s, 1)

                def norm_var(mv_, veps_, s, s_out_):
                    dve.wait_ge(s, 1)
                    dve.sem_inc(s, -1)
                    nc.vector.tensor_scalar_add(veps_[:], mv_[:, :, 1], EPS).then_inc(s_out_, 1)

                def norm_apply(base, n, mv_, rstd_, out_, s_in, s):
                    dve.wait_ge(s_in, 1)
                    dve.sem_inc(s_in, -1)
                    for j in range(n):
                        last = nc.vector.tensor_scalar(out_[:, j, :], x[:, ds(base + j * P, P)], mv_[:, j, 0:1],
                                                       rstd_[:, j:j + 1], ALU.subtract, ALU.mult)
                    last.then_inc(s, 1)

                def split_h(par):
                    dve.wait_ge(s_hfd, 1)
                    dve.sem_inc(s_hfd, -1)
                    nc.vector.tensor_tensor(hl[par][:, 1, :], hf[par][:, 1, :], hh[par][:, 1, :],
                                            ALU.subtract).then_inc(s_h[1], 1)

                def weigh(t, par, e):
                    dve.wait_ge(s_y, 1)
                    dve.sem_inc(s_y, -1)
                    dve.wait_ge(s_x, 1)
                    dve.sem_inc(s_x, -1)
                    for j in range(TB):
                        xs = x[:, ds(t * TT + j * P, P)]
                        last = nc.vector.scalar_tensor_tensor(out=xs, in0=b_y[:, j * P:(j + 1) * P],
                                                              scalar=cw[par][:, j, e:e + 1], in1=xs,
                                                              op0=ALU.mult, op1=ALU.add)
                    last.then_inc(s_acc, 1)
                    mark()

                S, W = small, wide

                def row(i):
                    return S[:, i, :]

                def over(i):
                    return S[:, i, :].unsqueeze(2).to_broadcast([P, TB, E])

                LG = b_ring[1][:, 0:TB * E].rearrange("p (j e) -> p j e", e=E)

                def gate_max():
                    dve.wait_ge(s_ring_d, 1)
                    dve.sem_inc(s_ring_d, -1)
                    nc.vector.reduce_max(row(0), LG, AX.X).then_inc(s_gate, 1)

                def gate_shift():
                    dve.wait_ge(s_gate, 1)
                    dve.sem_inc(s_gate, -1)
                    nc.vector.tensor_tensor(W[:, 0], LG, over(0), ALU.subtract).then_inc(s_shift, 1)
                    nc.vector.memset(spare[:, 3:4], 0.0).then_inc(s_free[1], 1)

                def gate_sum():
                    dve.wait_ge(s_exp, 1)
                    dve.sem_inc(s_exp, -1)
                    nc.vector.reduce_sum(row(1), W[:, 1], AX.X).then_inc(s_gate, 1)

                def gate_inverse():
                    dve.wait_ge(s_gate, 1)
                    dve.sem_inc(s_gate, -1)
                    nc.vector.reciprocal(row(2), row(1)).then_inc(s_gate, 1)

                def gate_probs():
                    dve.wait_ge(s_gate, 1)
                    dve.sem_inc(s_gate, -1)
                    nc.vector.tensor_tensor(W[:, 2], W[:, 1], over(2), ALU.mult).then_inc(s_gate, 1)

                def largest(src, top):
                    dve.wait_ge(s_gate, 1)
                    dve.sem_inc(s_gate, -1)
                    nc.vector.reduce_max(row(top), W[:, src], AX.X).then_inc(s_gate, 1)

                def equals(src, top, equal):
                    dve.wait_ge(s_gate, 1)
                    dve.sem_inc(s_gate, -1)
                    nc.vector.tensor_tensor(W[:, equal], W[:, src], over(top), ALU.is_equal).then_inc(s_gate, 1)

                def ranks(equal, rank):
                    dve.wait_ge(s_gate, 1)
                    dve.sem_inc(s_gate, -1)
                    nc.vector.tensor_tensor(W[:, rank], W[:, equal], order[:], ALU.mult).then_inc(s_gate, 1)

                def gate_rest():
                    dve.wait_ge(s_gate, 1)
                    dve.sem_inc(s_gate, -1)
                    nc.vector.scalar_tensor_tensor(out=W[:, 6], in0=W[:, 5], scalar=-2.0, in1=W[:, 2],
                                                   op0=ALU.mult, op1=ALU.add).then_inc(s_gate, 1)

                def gate_total():
                    dve.wait_ge(s_gate, 1)
                    dve.sem_inc(s_gate, -1)
                    nc.vector.scalar_tensor_tensor(out=row(7), in0=row(3), scalar=1e-8, in1=row(5),
                                                   op0=ALU.add, op1=ALU.add)
                    nc.vector.tensor_tensor(W[:, 3], W[:, 5], W[:, 9], ALU.add).then_inc(s_gate, 1)

                def gate_keep():
                    dve.wait_ge(s_gate, 1)
                    dve.sem_inc(s_gate, -1)
                    nc.vector.reciprocal(row(8), row(7))
                    nc.vector.tensor_tensor(W[:, 4], W[:, 2], W[:, 3], ALU.mult).then_inc(s_gate, 1)

                def gate_half():
                    dve.wait_ge(s_gate, 1)
                    dve.sem_inc(s_gate, -1)
                    nc.vector.scalar_tensor_tensor(out=half[:], in0=W[:, 4], scalar=0.5, in1=over(8),
                                                   op0=ALU.mult, op1=ALU.mult).then_inc(s_gate, 1)

                def gate_parts(par):
                    dve.wait_ge(s_gate, 1)
                    dve.sem_inc(s_gate, -1)
                    nc.vector.tensor_copy(cw3[:, :, 0, 0:E], half[:])
                    nc.vector.tensor_copy(cw3[:, :, 2, 0:E], half[:])
                    nc.vector.tensor_scalar(cw[par][:], half[:], 1.0 / (WS * WS), None,
                                            ALU.mult).then_inc(s_gate, 1)

                def gate_low():
                    dve.wait_ge(s_gate, 1)
                    dve.sem_inc(s_gate, -1)
                    nc.vector.tensor_tensor(cw3[:, :, 1, 0:E], half[:], cw3[:, :, 0, 0:E],
                                            ALU.subtract).then_inc(s_cw, 1)

                def f_init(t):
                    dve.wait_ge(s_x, 1)
                    dve.sem_inc(s_x, -1)
                    xs = x[:, ds(t * TT, TT)]
                    nc.vector.scalar_tensor_tensor(out=xs, in0=xn[:].rearrange("p j d -> p (j d)"), scalar=0.5,
                                                   in1=xs, op0=ALU.mult, op1=ALU.add).then_inc(s_x, 1)

                def f_bias(t):
                    dve.wait_ge(s_ring_d, 1)
                    dve.sem_inc(s_ring_d, -1)
                    dve.wait_ge(s_x, 1)
                    dve.sem_inc(s_x, -1)
                    xs = x[:, ds(t * TT, TT)]
                    nc.vector.scalar_tensor_tensor(out=xs, in0=b_ring[1][:, :], scalar=1.0 / (WS * WS), in1=xs,
                                                   op0=ALU.mult, op1=ALU.add).then_inc(s_free[1], 1)
                    mark()

                def a_max(r, part, bank):
                    dve.wait_ge(s_ring_d, 1)
                    dve.sem_inc(s_ring_d, -1)
                    s = b_ring[bank][:, :].rearrange("p (i k) -> p i k", k=SEQ)
                    nc.vector.reduce_max(mx[:, 1, NG * r + 2 * part - 2:NG * r + 2 * part], s,
                                         AX.X).then_inc(s_free[bank], 1)

                def a_mask(r, bank):
                    dve.wait_ge(s_ring_d, 1)
                    dve.sem_inc(s_ring_d, -1)
                    nc.vector.tensor_tensor(masked[:, r], b_ring[bank][:, :].rearrange("p (i k) -> p i k", k=P),
                                            mask[:], ALU.add).then_inc(s_free[bank], 1)
                    nc.vector.memset(spare[:, 4 + r:5 + r], 0.0).then_inc(s_masked, 1)

                def a_max_masked(r):
                    dve.wait_ge(s_masked, 1)
                    dve.sem_inc(s_masked, -1)
                    nc.vector.reduce_max(mx[:, 0, NG * r:NG * r + NG], masked[:, r], AX.X)

                def a_marr():
                    nc.vector.memset(spare[:, 1:2], 0.0).then_inc(s_dve, 1)
                    dve.wait_ge(s_dve, 1)
                    dve.sem_inc(s_dve, -1)
                    for j in range(SB):
                        last = nc.vector.tensor_scalar(marr[:, j, :, :, SLOT],
                                                       mx[:, j, :].rearrange("p (r g) -> p g r", g=NG),
                                                       -1.0, None, ALU.mult)
                    last.then_inc(s_marr, 1)

                def a_m(par, u):
                    dve.wait_ge(s_ring_d, 1)
                    dve.sem_inc(s_ring_d, -1)
                    q = qs[par][:, 2 * u:2 * u + 2, :].rearrange("p g t -> p (g t)")
                    nc.vector.tensor_tensor(q, q, b_ring[u][:, :], ALU.add).then_inc(s_free[u], 1)

                CT = b_pv[:, SEQ:2 * SEQ].rearrange("p (n h c) -> p n h c", h=2, c=16)

                def a_inverse():
                    dve.wait_ge(s_ct, 1)
                    dve.sem_inc(s_ct, -1)
                    nc.vector.reciprocal(rden[:], CT[:, :, :, HD]).then_inc(s_div, 1)

                def a_divide(k):
                    dve.wait_ge(s_div, 1)
                    dve.sem_inc(s_div, -1)
                    nc.vector.tensor_tensor(cn[:].rearrange("p (n k h d) -> p n k h d", k=2, h=2, d=HD)[:, :, k],
                                            CT[:, :, :, 0:HD],
                                            rden[:].unsqueeze(3).to_broadcast([P, SB * NG, 2, HD]),
                                            ALU.mult).then_inc(s_cn, 1)

                def a_residual(b):
                    dve.wait_ge(s_ring_d, 1)
                    dve.sem_inc(s_ring_d, -1)
                    dve.wait_ge(s_x, 1)
                    dve.sem_inc(s_x, -1)
                    xs = x[:, ds(b * SEQ, SEQ)]
                    nc.vector.tensor_tensor(xs, b_ring[1][:, 0:SEQ], xs, ALU.add).then_inc(s_free[1], 1)
                    mark()

                def split_w(n):
                    dve.wait_ge(s_wh[n], 1)
                    w, wf = ((w1, w1f), (w2, w2f))[n]
                    nc.vector.scalar_tensor_tensor(out=w[1][:], in0=wf[:], scalar=WS, in1=w[0][:],
                                                   op0=ALU.mult, op1=ALU.subtract).then_inc(s_wl[n], 1)

                def step(st):
                    m, f = st.maxima, st.nxt is not None
                    other, new = 1 - st.par, 1 - st.buf

                    def expert(s):
                        if st.alone and st.fore[s] is not None and st.fore[s][1] > 1:
                            split_h(st.fore[s][1] % 2)
                        if st.run[s] is not None:
                            weigh(st.cur, st.buf, st.run[s])

                    if st.tail:
                        a_inverse()
                    if m:
                        a_max(0, 2, 0)
                    if st.tail:
                        a_divide(1)
                    expert(0)
                    if m:
                        a_mask(0, 0)
                    if st.proj:
                        norm_stats((st.b + 2) * SEQ, SB, a_stats, s_anorm)
                        norm_aggr(SB, a_stats, a_mv, s_anorm)
                        norm_var(a_mv, a_veps, s_anorm, s_avar)
                    if m:
                        a_max(0, 1, 0)
                    if st.tail:
                        a_residual(st.b - 1)
                    if st.proj:
                        norm_apply((st.b + 2) * SEQ, SB, a_mv, a_rstd, a_xn, s_arstd, s_axn)
                    expert(1)
                    if m:
                        a_mask(1, 0)
                        a_max(1, 1, 1)
                    if f:
                        if st.load:
                            dve.wait_ge(s_xin, st.nxt * 16 + 16)
                            nc.vector.memset(spare[:, 2:3], 0.0).then_inc(s_dve, 1)
                            dve.wait_ge(s_dve, 1)
                            dve.sem_inc(s_dve, -1)
                        norm_stats(st.nxt * TT, TB, stats, s_norm)
                    if m:
                        a_max(1, 2, 0)
                    if f:
                        norm_aggr(TB, stats, mv, s_norm)
                    if f:
                        norm_var(mv, veps, s_norm, s_var)
                    if st.proj:
                        dve.wait_ge(s_axTh, 1)
                        dve.sem_inc(s_axTh, -1)
                        nc.vector.tensor_tensor(a_xTl[:], b_ring[1][:, 0:SEQ], a_xTh[:],
                                                ALU.subtract).then_inc(s_free[1], 1)
                    expert(2)
                    if m:
                        a_mask(2, 0)
                        a_max(2, 1, 1)
                    if f:
                        norm_apply(st.nxt * TT, TB, mv, rstd, xn, s_rstd, s_xn)
                    if st.opening == 1:
                        split_w(0)
                    if m:
                        a_max(2, 2, 0)
                    if st.proj:
                        dve.wait_ge(s_qkh, 1)
                        dve.sem_inc(s_qkh, -1)
                        nc.vector.scalar_tensor_tensor(out=qkl[:].rearrange("p a t -> p (a t)"),
                                                       in0=b_ring[1][:, :], scalar=1.0 / WS,
                                                       in1=qkh[:].rearrange("p a t -> p (a t)"),
                                                       op0=ALU.mult, op1=ALU.subtract).then_inc(s_free[1], 1)
                    expert(3)
                    if m:
                        a_max_masked(0)
                        a_mask(3, 0)
                    if f:
                        dve.wait_ge(s_xTh, 1)
                        dve.sem_inc(s_xTh, -1)
                        nc.vector.tensor_tensor(xTl[new][:], b_ring[1][:, :], xTh[new][:],
                                                ALU.subtract).then_inc(s_free[1], 1)
                    if st.here:
                        a_inverse()
                    if m:
                        a_max(3, 1, 0)
                    if st.here:
                        a_divide(0)
                    if m:
                        a_max_masked(1)
                    if f:
                        gate_max()
                    expert(4)
                    if f:
                        gate_shift()
                    if m:
                        a_max(3, 2, 0)
                        a_max_masked(2)
                    if f:
                        gate_sum()
                    if st.opening == 1:
                        split_w(1)
                    if f:
                        gate_inverse()
                    if m:
                        a_max_masked(3)
                    if f:
                        gate_probs()
                    if m:
                        a_marr()
                    if f:
                        largest(2, 3)
                    expert(5)
                    if f:
                        equals(2, 3, 3)
                    if f:
                        ranks(3, 4)
                    if st.cur is not None:
                        f_bias(st.cur)
                    if f:
                        largest(4, 4)
                    if m:
                        a_m(other, 0)
                        a_m(other, 1)
                    expert(6)
                    if st.opening == 2:
                        dve.wait_ge(w_in[3], 64)
                        nc.vector.tensor_scalar(wa[0][:], waf[:], WS, None, ALU.mult).then_inc(s_dve, 1)
                        dve.wait_ge(s_dve, 1)
                        dve.sem_inc(s_dve, -1)
                        nc.vector.scalar_tensor_tensor(out=wa[1][:], in0=waf[:], scalar=WS, in1=wa[0][:],
                                                       op0=ALU.mult, op1=ALU.subtract).then_inc(s_wa, 1)
                    if f:
                        equals(4, 4, 5)
                        gate_rest()
                        largest(6, 5)
                        equals(6, 5, 7)
                        ranks(7, 8)
                        largest(8, 6)
                        equals(8, 6, 9)
                        gate_total()
                        gate_keep()
                        gate_half()
                        gate_parts(new)
                        gate_low()
                    expert(7)
                    if f:
                        f_init(st.nxt)

                for s in s_free + [s_acc, s_cn, s_x]:
                    dve.sem_inc(s, 1)
                run_all(dve, step)

            @block.gpsimd
            def _(pool):
                def rsqrt(s_in, out_, in_, n, s):
                    pool.wait_ge(s_in, 1)
                    pool.sem_inc(s_in, -1)
                    nc.gpsimd.tensor_tensor(out_[:], in_[:], neg_half[:, 0:n], ALU.pow).then_inc(s, 1)

                def split_h(par, halves):
                    for c in halves:
                        pool.wait_ge(s_hf[c], 1)
                        pool.sem_inc(s_hf[c], -1)
                        nc.gpsimd.tensor_tensor(hl[par][:, c, :], hf[par][:, c, :], hh[par][:, c, :],
                                                ALU.subtract).then_inc(s_h[c], 1)

                def causal(r, part):
                    pool.wait_ge(s_e, 1)
                    pool.sem_inc(s_e, -1)
                    n, w = (4, P) if part == 2 else (2, SEQ)
                    v = pt[r % 2][:, part, :].rearrange("p (i q) -> p i q", q=w)[:, :, 0:P]
                    nc.gpsimd.affine_select(out=v, in_=v, compare_op=ALU.is_ge, fill=0.0, base=0,
                                            pattern=[[0, n], [1, P]], channel_multiplier=-1).then_inc(s_p, 1)

                def step(st):
                    for s in range(E):
                        if s % 2 == 0 and st.here:
                            causal(s // 2, 0)
                        if st.fore[s] is not None:
                            e = st.fore[s][1]
                            split_h(e % 2, (0,) if st.alone and e > 1 else (0, 1))
                        if s == 2 and st.nxt is not None:
                            rsqrt(s_var, rstd, veps, TB, s_rstd)
                        if s % 2 == 0 and st.here:
                            causal(s // 2, 1)
                            causal(s // 2, 2)
                        if s == 0 and st.proj:
                            rsqrt(s_avar, a_rstd, a_veps, SB, s_arstd)

                for c in range(HC):
                    pool.sem_inc(s_h[c], 1)
                pool.sem_inc(s_p, 2)
                run_all(pool, step)


_INS = ['L0_attn_x', 'L0_attn_q_proj', 'L0_attn_k_proj', 'L0_attn_v_proj', 'L0_attn_out_proj', 'L0_ffn_gate_W',
        'L0_ffn_W1', 'L0_ffn_b1', 'L0_ffn_W2', 'L0_ffn_b2']
_OUTS = [((32, 256, 128), 'float32')]


def kernel(**inputs):
    import numpy as _np
    import concourse.bacc as _bacc
    from concourse import mybir as _mybir
    from concourse.bass_utils import run_bass_kernel_spmd as _run

    nc = _bacc.Bacc("TRN2", target_bir_lowering=False, num_devices=1)
    arrays, args = {}, []
    for name in _INS:
        a = _np.ascontiguousarray(inputs[name])
        arrays[f"in_{name}_dram"] = a
        args.append(nc.dram_tensor(f"in_{name}_dram", a.shape, _mybir.dt.from_np(a.dtype), kind="ExternalInput").ap())
    for i, (shape, dtype) in enumerate(_OUTS):
        dt = _mybir.dt.from_np(_np.dtype(dtype))
        args.append(nc.dram_tensor(f"out_{i}_dram", shape, dt, kind="ExternalOutput").ap())
    build(nc, *args)
    r = _run(nc, [arrays], core_ids=[0])
    return r.results[0]["out_0_dram"]
```
